# Optimizing a Trainium2 kernel written in Bass

```python
import numpy as np
import jax
import jax.numpy as jnp

def _softmax(x, axis=-1):
    return jax.nn.softmax(x, axis=axis)

def _gelu(x):
    return jax.nn.gelu(x, approximate=True)

def _silu(x):
    return jax.nn.silu(x)

def _sigmoid(x):
    return jax.nn.sigmoid(x)

def _layernorm(x, axis=-1, eps=1e-05):
    m = jnp.mean(x, axis=axis, keepdims=True)
    v = jnp.var(x, axis=axis, keepdims=True)
    return (x - m) / jnp.sqrt(v + eps)

def _scatter_add(tgt, idx, src, axis=0):
    return tgt.at[idx].add(src)

def _segment_sum(src, seg, n):
    return jax.ops.segment_sum(src, seg, n)
kernel_name = 'mk_gps_d1_gnn_r8_c9d666'

def setup_inputs(seed: int=0):
    np.random.seed(seed)
    _w = jnp.asarray

    def _rec_inputs():
        import jax
        import jax.numpy as jnp
        _gk = jax.random.key(seed)
        x = -0.0003713 + 1 * jax.random.normal(jax.random.fold_in(_gk, 1), (6250, 256), jnp.float32)
        _s = jax.random.randint(jax.random.fold_in(_gk, 2), (50000,), 0, 6250, jnp.int32)
        _d = jax.random.randint(jax.random.fold_in(_gk, 3), (50000,), 0, 6250, jnp.int32)
        _loop = jnp.arange(6250, dtype=jnp.int32)
        src = jnp.concatenate([_s, _d, _loop])
        dst = jnp.concatenate([_d, _s, _loop])
        _o = jnp.argsort(dst, stable=True)
        src = src[_o]
        dst = dst[_o]
        edge_attr_194 = 0.000189139 + 1.00015 * jax.random.normal(jax.random.fold_in(_gk, 11), (106250, 194), jnp.float32)
        return (x, src, dst, edge_attr_194)
    x, src, dst, edge_attr_194 = _rec_inputs()

    def _L0_gnn_setup():
        import jax, jax.numpy as jnp
        import numpy as np
        N = 6250
        E = 31250
        IN = 256
        OUT = 256
        H = 4
        C = OUT // H
        MSG = 128
        TIME = 64
        ED = MSG + TIME + 2

        def _glorot(k, shape):
            return (jax.random.normal(k, shape, jnp.float32) / np.sqrt(shape[0])).astype(jnp.float32)

        def _tconv(x, src, dst, edge_attr, Wq, bq, Wk, bk, Wv, bv, We, Ws, bs):
            n = x.shape[0]
            q = (x @ Wq + bq).reshape(n, H, C)
            k = (x @ Wk + bk).reshape(n, H, C)
            v = (x @ Wv + bv).reshape(n, H, C)
            e = (edge_attr @ We).reshape(-1, H, C)
            kj = k[src] + e
            vj = v[src] + e
            logits = jnp.einsum('ehc,ehc->eh', q[dst], kj) / np.sqrt(C)
            m = jax.lax.stop_gradient(jax.ops.segment_max(logits, dst, num_segments=n))
            ex = jnp.exp(logits - m[dst])
            denom = jax.ops.segment_sum(ex, dst, num_segments=n)
            a = ex / (denom[dst] + 1e-16)
            agg = jax.ops.segment_sum(vj * a[:, :, None], dst, num_segments=n)
            return agg.reshape(n, H * C) + x @ Ws + bs
        ks = jax.random.split(jax.random.key(seed), 16)
        z = lambda: jnp.zeros((H * C,), jnp.float32)
        inp = {'x': jax.random.normal(ks[0], (N, IN), jnp.float32), 'edge_index': jax.random.randint(ks[1], (2, E), 0, N), 'edge_attr': jax.random.normal(ks[2], (E, ED), jnp.float32), 'Wq1': _glorot(ks[3], (IN, H * C)), 'bq1': z(), 'Wk1': _glorot(ks[4], (IN, H * C)), 'bk1': z(), 'Wv1': _glorot(ks[5], (IN, H * C)), 'bv1': z(), 'We1': _glorot(ks[6], (ED, H * C)), 'Ws1': _glorot(ks[7], (IN, H * C)), 'bs1': z(), 'Wq2': _glorot(ks[8], (OUT, H * C)), 'bq2': z(), 'Wk2': _glorot(ks[9], (OUT, H * C)), 'bk2': z(), 'Wv2': _glorot(ks[10], (OUT, H * C)), 'bv2': z(), 'We2': _glorot(ks[11], (ED, H * C)), 'Ws2': _glorot(ks[12], (OUT, H * C)), 'bs2': z()}
        return inp
    _L0_gnn_all = _L0_gnn_setup()
    _L0_gnn_in = {k: v for k, v in _L0_gnn_all.items() if k in ('Wq1', 'bq1', 'Wk1', 'bk1', 'Wv1', 'bv1', 'We1', 'Ws1', 'bs1', 'Wq2', 'bq2', 'Wk2', 'bk2', 'Wv2', 'bv2', 'We2', 'Ws2', 'bs2')}
    del _L0_gnn_all

    def _L0_mix_setup():
        import jax, jax.numpy as jnp
        import numpy as np
        HEADS = 4
        DIM_HEAD = 32
        key = jax.random.key(seed)
        k1, k2, k3 = jax.random.split(key, 3)
        B, L, D = (16, 1024, 256)
        hidden = HEADS * DIM_HEAD
        x = jax.random.normal(k1, (B, L, D), dtype=jnp.float32)
        W_qkv = jax.random.normal(k2, (D, 3 * hidden), dtype=jnp.float32) * D ** (-0.5)
        W_out = jax.random.normal(k3, (hidden, D), dtype=jnp.float32) * hidden ** (-0.5)
        b_out = jnp.zeros((D,), dtype=jnp.float32)
        return {'x': x, 'W_qkv': W_qkv, 'W_out': W_out, 'b_out': b_out}
    _L0_mix_all = _L0_mix_setup()
    _L0_mix_in = {k: v for k, v in _L0_mix_all.items() if k in ('W_qkv', 'W_out', 'b_out')}
    del _L0_mix_all

    def _L0_ffn_setup():
        import jax, jax.numpy as jnp
        import numpy as np
        E = 8
        K = 2
        D = 256
        H = 512
        DOUT = 256
        EPS = 1e-05
        key = jax.random.key(seed)
        ks = jax.random.split(key, 9)
        s = 0.02
        return {'x': jax.random.normal(ks[0], (4, 1024, D), jnp.float32), 'gamma': 1.0 + 0.05 * jax.random.normal(ks[1], (D,), jnp.float32), 'beta': 0.05 * jax.random.normal(ks[2], (D,), jnp.float32), 'Wr': 0.01 * jax.random.normal(ks[3], (D, E), jnp.float32), 'br': jnp.zeros((E,), jnp.float32), 'W1': s * jax.random.normal(ks[4], (E, D, H), jnp.float32), 'b1': s * jax.random.normal(ks[5], (E, H), jnp.float32), 'W2': s * jax.random.normal(ks[6], (E, H, DOUT), jnp.float32), 'b2': s * jax.random.normal(ks[7], (E, DOUT), jnp.float32)}
    _L0_ffn_all = _L0_ffn_setup()
    _L0_ffn_in = {k: v for k, v in _L0_ffn_all.items() if k in ('gamma', 'beta', 'Wr', 'br', 'W1', 'b1', 'W2', 'b2')}
    del _L0_ffn_all
    return {'x': x, 'src': src, 'dst': dst, 'edge_attr_194': edge_attr_194, 'L0_gnn_Wq1': _L0_gnn_in['Wq1'], 'L0_gnn_bq1': _L0_gnn_in['bq1'], 'L0_gnn_Wk1': _L0_gnn_in['Wk1'], 'L0_gnn_bk1': _L0_gnn_in['bk1'], 'L0_gnn_Wv1': _L0_gnn_in['Wv1'], 'L0_gnn_bv1': _L0_gnn_in['bv1'], 'L0_gnn_We1': _L0_gnn_in['We1'], 'L0_gnn_Ws1': _L0_gnn_in['Ws1'], 'L0_gnn_bs1': _L0_gnn_in['bs1'], 'L0_gnn_Wq2': _L0_gnn_in['Wq2'], 'L0_gnn_bq2': _L0_gnn_in['bq2'], 'L0_gnn_Wk2': _L0_gnn_in['Wk2'], 'L0_gnn_bk2': _L0_gnn_in['bk2'], 'L0_gnn_Wv2': _L0_gnn_in['Wv2'], 'L0_gnn_bv2': _L0_gnn_in['bv2'], 'L0_gnn_We2': _L0_gnn_in['We2'], 'L0_gnn_Ws2': _L0_gnn_in['Ws2'], 'L0_gnn_bs2': _L0_gnn_in['bs2'], 'L0_mix_W_qkv': _L0_mix_in['W_qkv'], 'L0_mix_W_out': _L0_mix_in['W_out'], 'L0_mix_b_out': _L0_mix_in['b_out'], 'L0_ffn_gamma': _L0_ffn_in['gamma'], 'L0_ffn_beta': _L0_ffn_in['beta'], 'L0_ffn_Wr': _L0_ffn_in['Wr'], 'L0_ffn_br': _L0_ffn_in['br'], 'L0_ffn_W1': _L0_ffn_in['W1'], 'L0_ffn_b1': _L0_ffn_in['b1'], 'L0_ffn_W2': _L0_ffn_in['W2'], 'L0_ffn_b2': _L0_ffn_in['b2']}

def reference(x, src, dst, edge_attr_194, L0_gnn_Wq1, L0_gnn_bq1, L0_gnn_Wk1, L0_gnn_bk1, L0_gnn_Wv1, L0_gnn_bv1, L0_gnn_We1, L0_gnn_Ws1, L0_gnn_bs1, L0_gnn_Wq2, L0_gnn_bq2, L0_gnn_Wk2, L0_gnn_bk2, L0_gnn_Wv2, L0_gnn_bv2, L0_gnn_We2, L0_gnn_Ws2, L0_gnn_bs2, L0_mix_W_qkv, L0_mix_W_out, L0_mix_b_out, L0_ffn_gamma, L0_ffn_beta, L0_ffn_Wr, L0_ffn_br, L0_ffn_W1, L0_ffn_b1, L0_ffn_W2, L0_ffn_b2):
    import jax
    import jax.numpy as jnp

    def _L0_gnn_ref(x, edge_index, edge_attr, Wq1, bq1, Wk1, bk1, Wv1, bv1, We1, Ws1, bs1, Wq2, bq2, Wk2, bk2, Wv2, bv2, We2, Ws2, bs2):
        import jax, jax.numpy as jnp
        import numpy as np
        N = 6250
        E = 31250
        IN = 256
        OUT = 256
        H = 4
        C = OUT // H
        MSG = 128
        TIME = 64
        ED = MSG + TIME + 2

        def _glorot(k, shape):
            return (jax.random.normal(k, shape, jnp.float32) / np.sqrt(shape[0])).astype(jnp.float32)

        def _tconv(x, src, dst, edge_attr, Wq, bq, Wk, bk, Wv, bv, We, Ws, bs):
            n = x.shape[0]
            q = (x @ Wq + bq).reshape(n, H, C)
            k = (x @ Wk + bk).reshape(n, H, C)
            v = (x @ Wv + bv).reshape(n, H, C)
            e = (edge_attr @ We).reshape(-1, H, C)
            kj = k[src] + e
            vj = v[src] + e
            logits = jnp.einsum('ehc,ehc->eh', q[dst], kj) / np.sqrt(C)
            m = jax.lax.stop_gradient(jax.ops.segment_max(logits, dst, num_segments=n))
            ex = jnp.exp(logits - m[dst])
            denom = jax.ops.segment_sum(ex, dst, num_segments=n)
            a = ex / (denom[dst] + 1e-16)
            agg = jax.ops.segment_sum(vj * a[:, :, None], dst, num_segments=n)
            return agg.reshape(n, H * C) + x @ Ws + bs
        src, dst = (edge_index[0], edge_index[1])
        h = jax.nn.relu(_tconv(x, src, dst, edge_attr, Wq1, bq1, Wk1, bk1, Wv1, bv1, We1, Ws1, bs1))
        return _tconv(h, src, dst, edge_attr, Wq2, bq2, Wk2, bk2, Wv2, bv2, We2, Ws2, bs2)

    def _L0_mix_ref(x, W_qkv, W_out, b_out):
        import jax, jax.numpy as jnp
        import numpy as np
        HEADS = 4
        DIM_HEAD = 32
        B, L, D = x.shape
        scale = DIM_HEAD ** (-0.5)
        qkv = jnp.einsum('bld,df->blf', x, W_qkv)
        qkv = qkv.reshape(B, L, 3, HEADS, DIM_HEAD)
        q = jnp.transpose(qkv[:, :, 0], (0, 2, 1, 3)) * scale
        k = jax.nn.softmax(jnp.transpose(qkv[:, :, 1], (0, 2, 1, 3)), axis=2)
        v = jnp.transpose(qkv[:, :, 2], (0, 2, 1, 3))
        context = jnp.einsum('bhld,bhle->bhde', k, v)
        out = jnp.einsum('bhde,bhld->bhle', context, q)
        out = jnp.transpose(out, (0, 2, 1, 3)).reshape(B, L, HEADS * DIM_HEAD)
        return jnp.einsum('blf,fd->bld', out, W_out) + b_out

    def _L0_ffn_ref(x, gamma, beta, Wr, br, W1, b1, W2, b2):
        import jax, jax.numpy as jnp
        import numpy as np
        E = 8
        K = 2
        D = 256
        H = 512
        DOUT = 256
        EPS = 1e-05
        mu = jnp.mean(x, axis=-1, keepdims=True)
        var = jnp.mean(jnp.square(x - mu), axis=-1, keepdims=True)
        xn = (x - mu) * jax.lax.rsqrt(var + EPS) * gamma + beta
        logits = jnp.einsum('bsd,de->bse', xn, Wr) + br
        top_vals, top_idx = jax.lax.top_k(logits, K)
        w = jax.nn.softmax(top_vals, axis=-1)
        w_full = jnp.einsum('bsk,bske->bse', w, jax.nn.one_hot(top_idx, E, dtype=w.dtype))
        y = jnp.zeros(x.shape[:-1] + (DOUT,), x.dtype)
        for e in range(E):
            h = jax.nn.gelu(jnp.einsum('bsd,dh->bsh', xn, W1[e]) + b1[e], approximate=False)
            y_e = jnp.einsum('bsh,hd->bsd', h, W2[e]) + b2[e]
            y = y + y_e * w_full[..., e, None]
        return y
    edge_index = jnp.stack([src, dst])
    xn = _layernorm(x, axis=-1)
    x = x + _L0_gnn_ref(xn, edge_index, edge_attr_194, L0_gnn_Wq1, L0_gnn_bq1, L0_gnn_Wk1, L0_gnn_bk1, L0_gnn_Wv1, L0_gnn_bv1, L0_gnn_We1, L0_gnn_Ws1, L0_gnn_bs1, L0_gnn_Wq2, L0_gnn_bq2, L0_gnn_Wk2, L0_gnn_bk2, L0_gnn_Wv2, L0_gnn_bv2, L0_gnn_We2, L0_gnn_Ws2, L0_gnn_bs2) + _L0_mix_ref(xn[None], L0_mix_W_qkv, L0_mix_W_out, L0_mix_b_out)[0]
    x = x + _L0_ffn_ref(_layernorm(x, axis=-1)[None], L0_ffn_gamma, L0_ffn_beta, L0_ffn_Wr, L0_ffn_br, L0_ffn_W1, L0_ffn_b1, L0_ffn_W2, L0_ffn_b2)[0]
    return x

_drawn_inputs = setup_inputs


def setup_inputs(seed=0):
    import zlib

    import numpy as np

    out = dict(_drawn_inputs(seed))
    spreads = {'L0_gnn_bq1': (0.0, 0.1),
     'L0_gnn_bk1': (0.0, 0.8),
     'L0_gnn_bv1': (0.0, 0.1),
     'L0_gnn_bs1': (0.0, 0.1),
     'L0_gnn_bq2': (0.0, 0.1),
     'L0_gnn_bk2': (0.0, 0.8),
     'L0_gnn_bv2': (0.0, 0.1),
     'L0_gnn_bs2': (0.0, 0.1),
     'L0_mix_b_out': (0.0, 0.1),
     'L0_ffn_br': (0.0, 0.1)}
    factors = {'L0_ffn_gamma': 8.0, 'L0_ffn_beta': 6.961, 'L0_ffn_b1': 8.0, 'L0_ffn_b2': 6.359}
    for name, (base, spread) in spreads.items():
        noise = np.random.default_rng([zlib.crc32(name.encode()), seed]).standard_normal(out[name].shape)
        drawn = base * np.exp(spread * noise) if base else spread * noise
        out[name] = jnp.asarray(drawn.astype(out[name].dtype))
    for name, factor in factors.items():
        out[name] = (out[name] * factor).astype(out[name].dtype)
    return out
```

```python
from contextlib import ExitStack

import concourse.bass as bass
from concourse import mybir

P = 128
D = 256
H = 4
C = D // H
ED = 194
EK = ED // 2
MH = 128
MC = 32
EX = 8
HID = 512
EPS = 1e-5
FAR = 1e30

F32 = mybir.dt.float32
I32 = mybir.dt.int32
U32 = mybir.dt.uint32
ALU = mybir.AluOpType
ACT = mybir.ActivationFunctionType
AX = mybir.AxisListType.X


class Record:
    pass


def sizes(n_nodes, n_edges):
    z = Record()
    z.N, z.E = n_nodes, n_edges
    z.NB = -(-n_nodes // P)
    z.NT = -(-n_edges // P)
    z.NT += -(z.NT + z.NB - 1) % 16
    z.NS = z.NT + z.NB - 1
    z.NSP = -(-z.NS // P) * P
    z.U = z.NSP // P
    z.G = z.NSP // 32
    z.NE = -(-(2 * z.NB + EX - 1) // 6) * 6
    z.UB = max(d for d in range(1, 8) if z.NB % d == 0)
    return z


class Stage:

    def __init__(self, nc, name):
        self.nc, self.name, self.ctx, self.sems = nc, name, ExitStack(), []

    def __enter__(self):
        return self

    def __exit__(self, *a):
        self.ctx.close()
        if self.sems:
            self.nc.clear_and_free_semaphores(self.sems)
            self.nc.all_engine_barrier()

    def sb(self, name, shape, dt=F32):
        return self.ctx.enter_context(self.nc.sbuf_tensor(f"{self.name}_{name}", shape, dt))

    def ps(self, name, shape, dt=F32):
        return self.ctx.enter_context(self.nc.psum_tensor(f"{self.name}_{name}", shape, dt))

    def sem(self, name):
        self.sems.append(self.nc.alloc_semaphore(f"{self.name}_{name}"))
        return self.sems[-1]

    def block(self):
        return self.ctx.enter_context(self.nc.Block())


def back(j, ring, unroll):
    return ring if j >= ring else j + unroll - max(k for k in range(unroll) if k % ring == j % ring)


def constants(nc, g):
    with Stage(nc, "const") as st:
        s_iota, s_f = st.sem("s_iota"), st.sem("s_cast")
        pi = st.sb("pi", [P, 1], I32)
        fi = st.sb("fi", [P, P], I32)
        block = st.block()

        @block.gpsimd
        def _(pool):
            nc.gpsimd.iota(pi[:, :], [[0, 1]], base=0, channel_multiplier=1).then_inc(s_iota, 1)
            nc.gpsimd.iota(fi[:, :], [[1, P]], base=0, channel_multiplier=0).then_inc(s_iota, 1)

        @block.vector
        def _(dve):
            dve.wait_ge(s_iota, 2)
            nc.vector.tensor_copy(g.part[:, :], pi[:, :]).then_inc(s_f, 1)
            nc.vector.tensor_copy(g.free[:, :], fi[:, :]).then_inc(s_f, 1)
            dve.wait_ge(s_f, 2)
            nc.vector.tensor_scalar(g.ident[:, :], g.free[:, :], g.part[:, 0:1], None, ALU.is_equal)
            nc.vector.memset(g.ones[:, :], 1.0)


def plan(nc, z, g, src_t, dst_t, dst_first):
    U, NSP, NT = z.U, z.NSP, z.NT
    with Stage(nc, "plan") as st:
        first = st.sb("first", [P, NT], I32)
        fblk = st.sb("fblk", [P, NT], I32)
        iot = st.sb("iot", [P, NT], I32)
        cross = st.sb("cross", [P, NT])
        hit = st.sb("hit", [P, NT])
        sidx = st.sb("sidx", [P, U], I32)
        sval = st.sb("sval", [P, U])
        tS = st.sb("tS", [P, U])
        bS = st.sb("bS", [P, U])
        b128 = st.sb("b128", [P, U])
        tI = st.sb("tI", [P, U], I32)
        bI = st.sb("bI", [P, U], I32)
        srcR = st.sb("srcR", [P, U, P], I32)
        dstR = st.sb("dstR", [P, U, P], I32)
        srcF = st.sb("srcF", [P, U, P])
        dstF = st.sb("dstF", [P, U, P])
        rel = st.sb("rel", [P, U, P])
        ok = st.sb("ok", [P, U, P])
        ok2 = st.sb("ok2", [P, U, P])
        key = st.sb("key", [P, U * P])
        kp = st.sb("kp", [P, U * P])
        kn = st.sb("kn", [P, U * P])
        edge = st.sb("edge", [1, 2])
        wp = st.sb("wp", [P, 2])
        wp4 = st.sb("wp4", [P, 2, H])
        pt = st.ps("pt", [P, 2, 4, P])
        pw = st.ps("pw", [H, 2, P])
        s_in, s_iota, s_c = st.sem("s_in"), st.sem("s_iota"), st.sem("s_c")
        s_tab, s_g, s_rel = st.sem("s_tab"), st.sem("s_g"), st.sem("s_rel")
        s_store, s_tr, s_ev, s_w, s_wt = (st.sem(n) for n in ("s_store", "s_tr", "s_ev", "s_w", "s_wt"))
        s_tst, s_tld, s_key = st.sem("s_tst"), st.sem("s_tld"), st.sem("s_key")
        NTR = 2 * U
        block = st.block()

        @block.sync
        def _(sp):
            sp.dma_start(first[:, :], dst_first.partition_broadcast(P)).then_inc(s_in, 16)
            sp.wait_ge(s_tab, 1)
            for r, tab in enumerate((tI, bI)):
                sp.dma_start(g.tabD[r, :].rearrange("(j p) -> p j", p=P), tab[:, :],
                             allow_slow_non_contiguous=True).then_inc(s_tst, 16)
            sp.wait_ge(s_tst, 32)
            sp.dma_start(g.tab[0:1, :], g.tabD.rearrange("r s -> (r s)").unsqueeze(0)).then_inc(s_tld, 16)
            sp.wait_ge(s_tld, 16)
            sp.wait_ge(s_rel, 1)
            sp.dma_start(g.relD.rearrange("(j p) e -> p j e", p=P), rel[:, :, :]).then_inc(s_store, 16)
            sp.dma_start(g.keyD[1:1 + NSP * P].rearrange("(j p e) -> p j e", p=P, e=P),
                         key[:, :].rearrange("p (j e) -> p j e", e=P)).then_inc(s_store, 16)
            sp.dma_start(g.keyD[0:1].unsqueeze(0), edge[:, 0:1]).then_inc(s_store, 16)
            sp.dma_start(g.keyD[1 + NSP * P:2 + NSP * P].unsqueeze(0), edge[:, 1:2]).then_inc(s_store, 16)
            sp.wait_ge(s_store, 64)
            for o, t in ((0, kp), (1, key), (2, kn)):
                sp.dma_start(t[:, :], g.keyD[o:o + NSP * P].rearrange("(p f) -> p f", p=P)).then_inc(s_key, 16)
            sp.wait_ge(s_key, 48)

        @block.gpsimd
        def _(pool):
            nc.gpsimd.iota(iot[:, :], [[1, NT]], base=0, channel_multiplier=0).then_inc(s_iota, 1)
            nc.gpsimd.iota(sidx[:, :], [[P, U]], base=0, channel_multiplier=1).then_inc(s_iota, 1)
            pool.wait_ge(s_tab, 1)
            for j in range(U):
                for tab, rows in ((src_t, srcR), (dst_t, dstR)):
                    nc.gpsimd.indirect_dma_start(
                        out=rows[:, j, :], out_offset=None, in_=tab,
                        in_offset=bass.IndirectOffsetOnAxis(ap=tI[:, j:j + 1].bitcast(U32), axis=0),
                    ).then_inc(s_g, 16)

        @block.vector
        def _(dve):
            n = [0]

            def link(ins):
                n[0] += 1
                ins.then_inc(s_c, 1)
                dve.wait_ge(s_c, n[0])

            dve.wait_ge(s_iota, 2)
            dve.wait_ge(s_in, 16)
            link(nc.vector.tensor_scalar(fblk[:, :], first[:, :], 7, None, ALU.arith_shift_right))
            link(nc.vector.tensor_tensor(cross[:, :], fblk[:, :], iot[:, :], ALU.add))
            link(nc.vector.tensor_copy(sval[:, :], sidx[:, :]))
            for j in range(U):
                link(nc.vector.tensor_scalar(hit[:, 1:NT], cross[:, 1:NT], sval[:, j:j + 1], None, ALU.is_le))
                link(nc.vector.tensor_reduce(tS[:, j:j + 1], hit[:, 1:NT], AX, ALU.add))
            link(nc.vector.tensor_tensor(bS[:, :], sval[:, :], tS[:, :], ALU.subtract))
            link(nc.vector.tensor_scalar(b128[:, :], bS[:, :], float(P), None, ALU.mult))
            link(nc.vector.tensor_copy(bI[:, :], bS[:, :]))
            link(nc.vector.memset(edge[:, :], -3.0))
            nc.vector.tensor_copy(tI[:, :], tS[:, :]).then_inc(s_tab, 1)
            dve.wait_ge(s_g, 32 * U)
            link(nc.vector.tensor_copy(srcF[:, :, :], srcR[:, :, :]))
            link(nc.vector.tensor_copy(dstF[:, :, :], dstR[:, :, :]))
            link(nc.vector.tensor_tensor(rel[:, :, :], dstF[:, :, :],
                                         b128[:, :].unsqueeze(2).to_broadcast([P, U, P]), ALU.subtract))
            link(nc.vector.tensor_scalar(ok[:, :, :], rel[:, :, :], 0.0, None, ALU.is_ge))
            link(nc.vector.tensor_scalar(ok2[:, :, :], rel[:, :, :], float(P), None, ALU.is_lt))
            link(nc.vector.tensor_tensor(ok[:, :, :], ok[:, :, :], ok2[:, :, :], ALU.mult))
            link(nc.vector.tensor_scalar(dstF[:, :, :], dstF[:, :, :], 2.0, None, ALU.add))
            link(nc.vector.tensor_tensor(dstF[:, :, :], dstF[:, :, :], ok[:, :, :], ALU.mult))
            link(nc.vector.tensor_scalar(key[:, :], dstF[:, :, :].rearrange("p j e -> p (j e)"), -2.0, None, ALU.add))
            nc.vector.sem_inc(s_rel, 1)
            for i in range(NTR):
                j, dst = i % U, (g.srcS, g.relS)[i // U]
                dve.wait_ge(s_tr, i + 1)
                nc.vector.tensor_copy(dst[:, j * P:(j + 1) * P], pt[:, i % 2, 0, :]).then_inc(s_ev, 1)
            dve.wait_ge(s_key, 48)
            for o, (t, pen) in enumerate(((kp, g.pen_prev), (kn, g.pen_next))):
                link(nc.vector.tensor_tensor(t[:, :], t[:, :], key[:, :], ALU.is_equal))
                link(nc.vector.tensor_scalar(pen[:, :], t[:, :], -1.0, FAR, ALU.add, ALU.mult))
                link(nc.vector.tensor_reduce(wp[:, o:o + 1], pen[:, :], AX, ALU.min))
            link(nc.vector.tensor_copy(wp4[:, :, :], wp[:, :].unsqueeze(2).to_broadcast([P, 2, H])))
            nc.vector.sem_inc(s_w, 1)
            dve.wait_ge(s_wt, 2)
            nc.vector.tensor_copy(g.pen_row[:, :, :], pw[:, :, :])

        @block.tensor
        def _(pe):
            pe.wait_ge(s_rel, 1)
            for i in range(NTR):
                j, rows = i % U, (srcF, rel)[i // U]
                if i >= 2:
                    pe.wait_ge(s_ev, i - 1)
                nc.tensor.transpose(pt[:, i % 2, 0, :], rows[:, j, :], g.ident[:, :]).then_inc(s_tr, 1)
            pe.wait_ge(s_w, 1)
            for o in range(2):
                nc.tensor.transpose(pw[:, o, :], wp4[:, o, :], g.ident[:, :]).then_inc(s_wt, 1)


def need(eng, sem, value):
    if not isinstance(value, int) or value > 0:
        eng.wait_ge(sem, value)


def turns(eng, n, body, peel=1):
    for i in range(min(peel, n)):
        body(i)
    if n > peel:
        with eng.Fori(peel, n) as i:
            body(i)


def nodes(nc, z, g, layer, a):
    UB, NB, one = z.UB, z.NB, layer == 1
    with Stage(nc, f"nodes{layer}") as st:
        W = st.sb("W", [P, 2, 4 * D])
        bias = st.sb("bias", [P, 4 * D])
        eps = st.sb("eps", [P, 1])
        xin = st.sb("xin", [P, UB, D])
        res = st.sb("res", [P, UB, D])
        stat = st.sb("stat", [P, UB, 6])
        mv = st.sb("mv", [P, UB, 2])
        sd = st.sb("sd", [P, UB])
        den = st.sb("den", [P, UB, H])
        rden = st.sb("rden", [P, UB, H])
        xn = st.sb("xn", [P, UB, D])
        hs = st.sb("hs", [P, UB, D])
        xT = st.sb("xT", [P, UB, 2, P])
        kvs = st.sb("kvs", [P, UB, 3 * D])
        pj = st.ps("pj", [P, 2, 4 * D])
        pT = st.ps("pT", [P, 2, 2 * D])
        pm = st.ps("pm", [P, 2, 4, P])
        if one:
            Wm = st.sb("Wm", [P, 2, 2 * MH])
        s_w, s_eps = st.sem("s_w"), st.sem("s_eps")
        s_x = [st.sem(f"s_x{j}") for j in range(UB)]
        s_r = [st.sem(f"s_r{j}") for j in range(UB)]
        s_st = [st.sem(f"s_st{j}") for j in range(UB)]
        s_xs = [st.sem(f"s_xs{j}") for j in range(UB)]
        s_stat, s_mv, s_sd, s_rs, s_xn, s_h1, s_h2 = (st.sem(n) for n in ("s_stat", "s_mv", "s_sd", "s_rs", "s_xn", "s_h1", "s_h2"))
        s_tr, s_xT, s_pj, s_ev, s_evm = (st.sem(n) for n in ("s_tr", "s_xT", "s_pj", "s_ev", "s_evm"))
        s_sk, s_step = st.sem("s_sk"), st.sem("s_step")
        NW = 4 + 4 + (1 if one else 0)
        block = st.block()

        @block.sync
        def _(sp):
            names = ["q", "k", "v", "s"]
            for n, w in enumerate(names):
                sp.dma_start(W[:, :, n * D:(n + 1) * D], a[f"W{w}{layer}"].rearrange("(c p) n -> p c n", p=P)).then_inc(s_w, 16)
                sp.dma_start(bias[:, n * D:(n + 1) * D], a[f"b{w}{layer}"].partition_broadcast(P)).then_inc(s_w, 16)
            if one:
                sp.dma_start(Wm[:, :, :], a["W_qkv"].rearrange("(c p) n -> p c n", p=P)[:, :, MH:3 * MH]).then_inc(s_w, 16)

            def body(i):
                for j in range(UB):
                    b = i * UB + j
                    need(sp, s_xn, b - UB + 1)
                    rows = bass.ds(b * P, P)
                    sp.dma_start(xin[:, j, :], (a["x"] if one else g.baseD)[rows, :]).then_inc(s_x[j], 16)
                    if not one:
                        need(sp, s_ev, b - UB + 1)
                        sp.dma_start(res[:, j, :], g.resD[rows, :]).then_inc(s_r[j], 16)
            turns(sp, NB // UB, body)

        @block.scalar
        def _(act):
            act.wait_ge(s_eps, 1)

            def store(i, j):
                b = i * UB + j
                act.wait_ge(s_ev, b + 1)
                act.dma_start(g.kvD[bass.ds(b * P, P), :], kvs[:, j, 0:2 * D]).then_inc(s_st[j], 16)
                act.dma_start((g.baseD if one else g.skipD)[bass.ds(b * P, P), :],
                              kvs[:, j, 2 * D:3 * D]).then_inc(s_st[j], 16)

            def body(i):
                if one:
                    act.wait_ge(s_mv, i + 1)
                    nc.scalar.activation(sd[:, :], mv[:, :, 1], ACT.Sqrt, bias=eps[:, 0:1]).then_inc(s_sd, 1)
                for j in range(UB):
                    b = i * UB + j
                    if not one:
                        act.wait_ge(s_h2, b + 1)
                        need(act, s_tr, b - UB + 1)
                        nc.scalar.activation(xn[:, j, :], hs[:, j, :], ACT.Relu).then_inc(s_xn, 1)
                for j in range(UB):
                    b = i * UB + j
                    act.wait_ge(s_tr, b + 1)
                    need(act, s_pj, b - UB + 1)
                    if one:
                        need(act, s_xs[j], 16 * i)
                    nc.scalar.activation(xT[:, j, :, :], pT[:, j % 2, 0:D].rearrange("p (c m) -> p c m", c=2), ACT.Copy).then_inc(s_xT, 1)
                    if one:
                        act.wait_ge(s_xT, b + 1)
                        act.dma_start(g.xTD[bass.ds(b * P, P), :], xT[:, j, :, :].rearrange("p c m -> p (c m)")).then_inc(s_xs[j], 16)
                        act.wait_ge(s_pj, b + 1)
                        nc.scalar.activation(g.kTm[:, bass.ds(b * P, P)], pm[:, j % 2, 0, :], ACT.Copy)
                        nc.scalar.activation(g.vm[:, bass.ds(b * P, P)], pm[:, j % 2, 1, :], ACT.Copy).then_inc(s_evm, 1)
                    if j >= 2:
                        store(i, j - 2)
                for j in range(max(UB - 2, 0), UB):
                    store(i, j)
            turns(act, NB // UB, body)
            for j in range(UB):
                act.wait_ge(s_st[j], 32 * (NB // UB))
                if one:
                    act.wait_ge(s_xs[j], 16 * (NB // UB))

        @block.tensor
        def _(pe):
            pe.wait_ge(s_w, 16 * NW)

            def transpose(i, j):
                b = i * UB + j
                pe.wait_ge(s_xn, b + 1)
                need(pe, s_xT, b - back(j, 2, UB) + 1)
                for c in range(2):
                    ins = nc.tensor.transpose(pT[:, j % 2, c * P:(c + 1) * P], xn[:, j, c * P:(c + 1) * P], g.ident[:, :])
                ins.then_inc(s_tr, 1)

            def body(i):
                transpose(i, 0)
                for j in range(UB):
                    b = i * UB + j
                    if j + 1 < UB:
                        transpose(i, j + 1)
                    pe.wait_ge(s_xT, b + 1)
                    need(pe, s_ev, b - back(j, 2, UB) + 1)
                    if one:
                        need(pe, s_evm, b - back(j, 2, UB) + 1)
                        for n in range(2):
                            for c in range(2):
                                l, r = Wm[:, c, n * MH:(n + 1) * MH], xT[:, j, c, :]
                                if n == 1:
                                    l, r = r, l
                                nc.tensor.matmul(pm[:, j % 2, n, :], l, r, start=(c == 0), stop=(c == 1))
                    for n in range(2):
                        for c in range(2):
                            ins = nc.tensor.matmul(pj[:, j % 2, n * 2 * D:(n + 1) * 2 * D], xT[:, j, c, :],
                                                   W[:, c, n * 2 * D:(n + 1) * 2 * D], start=(c == 0), stop=(c == 1))
                    ins.then_inc(s_pj, 1)
            turns(pe, NB // UB, body)

        @block.vector
        def _(dve):
            nc.vector.memset(eps[:, :], EPS).then_inc(s_eps, 1)
            dve.wait_ge(s_w, 16 * NW)

            def inputs(i):
                if one:
                    for j in range(UB):
                        dve.wait_ge(s_x[j], 16 * i + 16)
                        nc.vector.bn_stats(stat[:, j, :], xin[:, j, :]).then_inc(s_stat, 1)
                    dve.wait_ge(s_stat, (i + 1) * UB)
                    dve.sem_inc(s_step, 1)
                    for j in range(UB):
                        ins = nc.vector.bn_aggr(mv[:, j, :], stat[:, j, :])
                    ins.then_inc(s_mv, 1)
                    dve.wait_ge(s_sd, i + 1)
                    nc.vector.reciprocal(sd[:, :], sd[:, :]).then_inc(s_rs, 1)
                    dve.wait_ge(s_rs, i + 1)
                    for j in range(UB):
                        need(dve, s_tr, i * UB + j - UB + 1)
                        nc.vector.tensor_scalar(xn[:, j, :], xin[:, j, :], mv[:, j, 0:1], sd[:, j:j + 1],
                                                ALU.subtract, ALU.mult).then_inc(s_xn, 1)
                else:
                    at = g.acc[:, bass.ds(i * UB, UB), :]
                    nc.vector.tensor_scalar(den[:, :, :], at[:, :, D:D + H], 1e-16, None, ALU.add).then_inc(s_stat, 1)
                    dve.wait_ge(s_stat, i + 1)
                    nc.vector.reciprocal(rden[:, :, :], den[:, :, :]).then_inc(s_rs, 1)
                    dve.wait_ge(s_rs, i + 1)
                    for j in range(UB):
                        need(dve, s_xn, i * UB + j - UB + 1)
                        nc.vector.tensor_tensor(hs[:, j, :].rearrange("p (h c) -> p h c", h=H),
                                                g.acc[:, i * UB + j, 0:D].rearrange("p (h c) -> p h c", h=H) if isinstance(i, int) else
                                                g.acc[:, bass.ds(i * UB + j, 1), 0:D].rearrange("p o (h c) -> p (o h) c", h=H),
                                                rden[:, j, :].unsqueeze(2).to_broadcast([P, H, C]), ALU.mult).then_inc(s_h1, 1)
                    for j in range(UB):
                        dve.wait_ge(s_h1, i * UB + j + 1)
                        dve.wait_ge(s_x[j], 16 * i + 16)
                        nc.vector.tensor_tensor(hs[:, j, :], hs[:, j, :], xin[:, j, :], ALU.add).then_inc(s_h2, 1)

            def body(i):
                inputs(i)
                for j in range(UB):
                    b = i * UB + j
                    dve.wait_ge(s_pj, b + 1)
                    q = g.acc[:, bass.ds(b, 1), 0:D].rearrange("p o d -> p (o d)")
                    nc.vector.tensor_tensor(q, pj[:, j % 2, 0:D], bias[:, 0:D], ALU.add)
                    need(dve, s_st[j], 32 * i)
                    ins = nc.vector.tensor_tensor(kvs[:, j, :], pj[:, j % 2, D:4 * D], bias[:, D:4 * D], ALU.add)
                    if one:
                        ins.then_inc(s_ev, 1)
                    else:
                        ins.then_inc(s_sk, 1)
                        dve.wait_ge(s_sk, b + 1)
                        dve.wait_ge(s_r[j], 16 * i + 16)
                        nc.vector.tensor_tensor(kvs[:, j, 2 * D:3 * D], kvs[:, j, 2 * D:3 * D], res[:, j, :], ALU.add).then_inc(s_ev, 1)
            turns(dve, NB // UB, body)


def mix(nc, z, g, a):
    UB, NB, N = z.UB, z.NB, z.N
    with Stage(nc, "mix") as st:
        eb = st.sb("eb", [P, UB, P])
        ek = st.sb("ek", [P, UB, P])
        zero = st.sb("zero", [P, P])
        nmax = st.sb("nmax", [P, 1])
        es = st.sb("es", [P, NB])
        esum = st.sb("esum", [P, 1])
        rsum = st.sb("rsum", [P, 1])
        mask = st.sb("mask", [P, P])
        hrow = st.sb("hrow", [P, 2], I32)
        hcol = st.sb("hcol", [P, P], I32)
        rowf = st.sb("rowf", [P, 1])
        colf = st.sb("colf", [P, P])
        ctxm = st.sb("ctxm", [P, P])
        ctxT = st.sb("ctxT", [P, P])
        Wout = st.sb("Wout", [P, D])
        WqT = st.sb("WqT", [P, D])
        G = st.sb("G", [P, D])
        M = st.sb("M", [P, 2, D])
        bout = st.sb("bout", [P, D])
        xT = st.sb("xT", [P, UB, 2 * P])
        xin = st.sb("xin", [P, UB, D])
        xo = st.sb("xo", [P, UB, D])
        pe_ = st.ps("pe_", [P, 2, 4, P])
        pc = st.ps("pc", [P, 4, P])
        pg = st.ps("pg", [P, 3, 2 * D])
        po = st.ps("po", [P, 2, 2 * D])
        s_z, s_nm, s_eb, s_tr, s_ek, s_ctx, s_io, s_c, s_cm, s_ct, s_ctT, s_G, s_Gs, s_M, s_Ms, s_po, s_xo, s_w = (
            st.sem(n) for n in ("s_z", "s_nm", "s_eb", "s_tr", "s_ek", "s_ctx", "s_io", "s_c", "s_cm", "s_ct", "s_ctT",
                                "s_G", "s_Gs", "s_M", "s_Ms", "s_po", "s_xo", "s_w"))
        s_x = [st.sem(f"s_x{j}") for j in range(UB)]
        s_st = [st.sem(f"s_st{j}") for j in range(UB)]
        block = st.block()

        @block.sync
        def _(sp):
            sp.dma_start(Wout[:, :], a["W_out"]).then_inc(s_w, 16)
            sp.dma_start(WqT[:, :], a["Wq_mix_T"]).then_inc(s_w, 16)
            sp.dma_start(bout[:, :], a["b_out"].partition_broadcast(P)).then_inc(s_w, 16)

            def body(i):
                for j in range(UB):
                    b = i * UB + j
                    rows = bass.ds(b * P, P)
                    need(sp, s_po, b - UB + 1)
                    need(sp, s_xo, b - UB + 1)
                    sp.dma_start(xT[:, j, :], g.xTD[rows, :]).then_inc(s_x[j], 16)
                    sp.dma_start(xin[:, j, :], a["x"][rows, :]).then_inc(s_x[j], 16)
            turns(sp, NB // UB, body)

        @block.gpsimd
        def _(pool):
            nc.gpsimd.iota(hrow[:, :], [[0, 2]], base=0, channel_multiplier=1).then_inc(s_io, 1)
            nc.gpsimd.iota(hcol[:, :], [[1, P]], base=0, channel_multiplier=0).then_inc(s_io, 1)

        @block.scalar
        def _(act):
            act.wait_ge(s_nm, 1)

            def body(i):
                for j in range(UB):
                    b = i * UB + j
                    need(act, s_tr, b - UB + 1)
                    nc.scalar.activation(eb[:, j, :], g.kTm[:, bass.ds(b * P, P)], ACT.Exp, bias=nmax[:, 0:1],
                                         accum_out=es[:, bass.ds(b, 1)]).then_inc(s_eb, 1)
            turns(act, NB // UB, body)

            def out(i):
                for j in range(UB):
                    b = i * UB + j
                    act.wait_ge(s_xo, b + 1)
                    act.dma_start(g.resD[bass.ds(b * P, P), :], xo[:, j, :]).then_inc(s_st[j], 16)
            turns(act, NB // UB, out)
            for j in range(UB):
                act.wait_ge(s_st[j], 16 * (NB // UB))

        @block.tensor
        def _(pe):
            pe.wait_ge(s_z, 1)
            nc.tensor.matmul(pc[:, 0, :], zero[:, :], zero[:, :], start=True, stop=False)

            def body(i):
                for j in range(UB + 1):
                    if j < UB:
                        b = i * UB + j
                        pe.wait_ge(s_eb, b + 1)
                        need(pe, s_ek, b - back(j, 2, UB) + 1)
                        nc.tensor.transpose(pe_[:, j % 2, 0, :], eb[:, j, :], g.ident[:, :]).then_inc(s_tr, 1)
                    if j > 0:
                        b = i * UB + j - 1
                        pe.wait_ge(s_ek, b + 1)
                        nc.tensor.matmul(pc[:, 0, :], ek[:, j - 1, :], g.vm[:, bass.ds(b * P, P)],
                                         start=False, stop=False).then_inc(s_ctx, 1)
            turns(pe, NB // UB, body)
            nc.tensor.matmul(pc[:, 0, :], zero[:, :], zero[:, :], start=False, stop=True).then_inc(s_ctx, 1)
            pe.wait_ge(s_cm, 1)
            nc.tensor.transpose(pc[:, 1, :], ctxm[:, :], g.ident[:, :]).then_inc(s_ct, 1)
            pe.wait_ge(s_ctT, 1)
            pe.wait_ge(s_w, 48)
            nc.tensor.matmul(pg[:, 0, 0:D], ctxT[:, :], Wout[:, :], start=True, stop=True).then_inc(s_G, 1)
            pe.wait_ge(s_Gs, 1)
            for c in range(2):
                nc.tensor.matmul(pg[:, 1 + c, 0:D], WqT[:, c * P:(c + 1) * P], G[:, :], start=True, stop=True).then_inc(s_M, 1)
            pe.wait_ge(s_Ms, 1)

            def out(i):
                for j in range(UB):
                    b = i * UB + j
                    pe.wait_ge(s_x[j], 32 * i + 32)
                    need(pe, s_xo, b - back(j, 2, UB) + 1)
                    for c in range(2):
                        ins = nc.tensor.matmul(po[:, j % 2, 0:D], xT[:, j, c * P:(c + 1) * P], M[:, c, :],
                                               start=(c == 0), stop=(c == 1))
                    ins.then_inc(s_po, 1)
            turns(pe, NB // UB, out)

        @block.vector
        def _(dve):
            nc.vector.memset(zero[:, :], 0.0).then_inc(s_z, 1)
            if N < NB * P:
                nc.vector.memset(g.kTm[:, N:NB * P], -FAR)
            nc.vector.tensor_reduce(nmax[:, :], g.kTm[:, 0:N], AX, ALU.max, negate=True).then_inc(s_nm, 1)
            n = [0]

            def link(ins):
                n[0] += 1
                ins.then_inc(s_c, 1)
                dve.wait_ge(s_c, n[0])

            dve.wait_ge(s_io, 2)
            link(nc.vector.tensor_scalar(hrow[:, :], hrow[:, :], 5, None, ALU.arith_shift_right))
            link(nc.vector.tensor_scalar(hcol[:, :], hcol[:, :], 5, None, ALU.arith_shift_right))
            link(nc.vector.tensor_copy(rowf[:, :], hrow[:, 0:1]))
            link(nc.vector.tensor_copy(colf[:, :], hcol[:, :]))
            link(nc.vector.tensor_scalar(mask[:, :], colf[:, :], rowf[:, 0:1], MC ** -0.5, ALU.is_equal, ALU.mult))

            def body(i):
                for j in range(UB):
                    b = i * UB + j
                    dve.wait_ge(s_tr, b + 1)
                    need(dve, s_ctx, b - UB + 1)
                    nc.vector.tensor_copy(ek[:, j, :], pe_[:, j % 2, 0, :]).then_inc(s_ek, 1)
            turns(dve, NB // UB, body)
            dve.wait_ge(s_ctx, NB + 1)
            dve.wait_ge(s_eb, NB)
            link(nc.vector.tensor_reduce(esum[:, :], es[:, :], AX, ALU.add))
            link(nc.vector.reciprocal(rsum[:, :], esum[:, :]))
            nc.vector.scalar_tensor_tensor(out=ctxm[:, :], in0=pc[:, 0, :], scalar=rsum[:, 0:1], in1=mask[:, :],
                                           op0=ALU.mult, op1=ALU.mult).then_inc(s_cm, 1)
            dve.wait_ge(s_ct, 1)
            nc.vector.tensor_copy(ctxT[:, :], pc[:, 1, :]).then_inc(s_ctT, 1)
            dve.wait_ge(s_G, 1)
            nc.vector.tensor_copy(G[:, :], pg[:, 0, 0:D]).then_inc(s_Gs, 1)
            dve.wait_ge(s_M, 2)
            nc.vector.tensor_copy(M[:, :, :], pg[:, 1:3, 0:D]).then_inc(s_Ms, 1)
            dve.wait_ge(s_w, 48)

            def out(i):
                for j in range(UB):
                    b = i * UB + j
                    dve.wait_ge(s_x[j], 32 * i + 32)
                    need(dve, s_st[j], 16 * i)
                    link_x = nc.vector.tensor_tensor(xo[:, j, :], xin[:, j, :], bout[:, :], ALU.add)
                    link_x.then_inc(s_z, 1)
                for j in range(UB):
                    b = i * UB + j
                    dve.wait_ge(s_z, b + 2)
                    dve.wait_ge(s_po, b + 1)
                    nc.vector.tensor_tensor(xo[:, j, :], po[:, j % 2, 0:D], xo[:, j, :], ALU.add).then_inc(s_xo, 1)
            turns(dve, NB // UB, out)


def logits(nc, z, g, layer, a):
    T, HT = 16, 8
    NS = z.NS
    with Stage(nc, f"logits{layer}") as st:
        We = st.sb("We", [EK, 2, D])
        ea = st.sb("ea", [EK, T, 2, P])
        kb = st.sb("kb", [P, 2, HT * P])
        far = st.sb("far", [P, HT * P])
        npart = st.sb("npart", [P, 1])
        oht = st.sb("oht", [P, 2, HT * P])
        ix = st.sb("ix", [P, 2, HT], I32)
        kv = st.sb("kv", [P, T, 2 * D])
        kvj = st.sb("kvj", [P, 2, HT, 2, D])
        prod = st.sb("prod", [P, 4, D])
        ps = st.ps("ps", [P, HT, 2 * D])
        s_ea = [st.sem(f"s_ea{j}") for j in range(T)]
        s_kv = [st.sem(f"s_kv{j}") for j in range(T)]
        s_kb = [st.sem(f"s_kb{h}") for h in range(2)]
        s_vst = [st.sem(f"s_vst{h}") for h in range(2)]
        s_we, s_far, s_oht, s_ix, s_step, s_pe, s_add, s_prod, s_np = (
            st.sem(n) for n in ("s_we", "s_far", "s_oht", "s_ix", "s_step", "s_pe", "s_add", "s_prod", "s_np"))
        block = st.block()

        @block.sync
        def _(sp):
            sp.dma_start(We[:, :, :], a[f"We{layer}"].rearrange("(c p) n -> p c n", p=EK)).then_inc(s_we, 16)

            def body(i):
                for j in range(T):
                    s, h = i * T + j, j // HT
                    if j % HT == 0:
                        need(sp, s_far, 2 * (i - 1) + h + 1)
                        sp.dma_start(kb[:, h, :], g.relD[bass.ds(i * T + j, HT), :].rearrange("s e -> (s e)").partition_broadcast(P)).then_inc(s_kb[h], 16)
                    need(sp, s_pe, s - T + 1)
                    t = sp.value_load(g.tab[0:1, bass.ds(s, 1)], min_val=0, max_val=z.NT - 1)
                    sp.dma_start(ea[:, j, :, :].rearrange("p c e -> p (c e)"),
                                 a["ea_t"][bass.ds(t, 1), :, :].rearrange("o p n -> (o p) n")).then_inc(s_ea[j], 16)
            turns(sp, NS // T, body)

        @block.gpsimd
        def _(pool):
            if z.NSP > NS:
                nc.gpsimd.memset(g.L[:, NS:z.NSP, :], 0.0)

            def body(i):
                for h in range(2):
                    need(pool, s_add, (i - 1) * T + (h + 1) * HT)
                    nc.gpsimd.tensor_copy(ix[:, h, :], g.srcS[:, bass.ds(i * T + h * HT, HT)]).then_inc(s_ix, 1)
                    pool.wait_ge(s_ix, 2 * i + h + 1)
                    pool.sem_inc(s_step, 1)
                    for j in range(h * HT, (h + 1) * HT):
                        nc.gpsimd.indirect_dma_start(
                            out=kv[:, j, :], out_offset=None, in_=g.kvD,
                            in_offset=bass.IndirectOffsetOnAxis(ap=ix[:, h, j % HT:j % HT + 1].bitcast(U32), axis=0),
                        ).then_inc(s_kv[j], 16)
            turns(pool, NS // T, body)

        @block.scalar
        def _(act):
            act.wait_ge(s_np, 1)

            def onehot(i, h):
                act.wait_ge(s_kb[h], 16 * i + 16)
                need(act, s_oht, 2 * i + h)
                nc.scalar.activation(far[:, :], kb[:, h, :], ACT.Abs, bias=npart[:, 0:1]).then_inc(s_far, 1)
                act.wait_ge(s_far, 2 * i + h + 1)
                need(act, s_pe, (i - 1) * T + (h + 1) * HT)
                nc.scalar.activation(oht[:, h, :], far[:, :], ACT.Relu, bias=g.ones[:, 0:1], scale=-1.0).then_inc(s_oht, 1)

            def store(i, h):
                act.wait_ge(s_add, i * T + (h + 1) * HT)
                act.dma_start(g.vjD[bass.ds(2 * i + h, 1)].rearrange("o p t d -> (o p) t d"),
                              kvj[:, h, :, 1, :]).then_inc(s_vst[h], 16)

            def body(i):
                onehot(i, 0)
                if not isinstance(i, int) or i > 0:
                    store(i - 1, 1)
                onehot(i, 1)
                store(i, 0)
            turns(act, NS // T, body)
            store(NS // T - 1, 1)
            for h in range(2):
                act.wait_ge(s_vst[h], 16 * (NS // T))

        @block.tensor
        def _(pe):
            pe.wait_ge(s_we, 16)

            def body(i):
                for j in range(T):
                    s = i * T + j
                    b = pe.value_load(g.tab[0:1, bass.ds(z.NSP + s, 1)], min_val=0, max_val=z.NB - 1)
                    pe.wait_ge(s_ea[j], 16 * i + 16)
                    need(pe, s_prod, s - HT + 1)
                    for c in range(2):
                        nc.tensor.matmul(ps[:, j % HT, 0:D], ea[:, j, c, :], We[:, c, :], start=(c == 0), stop=(c == 1))
                    if j % HT == 0:
                        pe.wait_ge(s_oht, 2 * i + j // HT + 1)
                    nc.tensor.matmul(ps[:, j % HT, D:2 * D], oht[:, j // HT, (j % HT) * P:(j % HT + 1) * P],
                                     g.acc[:, bass.ds(b, 1), 0:D].rearrange("p o d -> p (o d)"), start=True, stop=True).then_inc(s_pe, 1)
            turns(pe, NS // T, body)

        @block.vector
        def _(dve):
            nc.vector.tensor_scalar(npart[:, :], g.part[:, :], -1.0, None, ALU.mult).then_inc(s_np, 1)

            def body(i):
                for j in range(T + 2):
                    s = i * T + j
                    if j < T:
                        dve.wait_ge(s_kv[j], 16 * i + 16)
                        dve.wait_ge(s_pe, s + 1)
                        if j % HT == 0:
                            need(dve, s_vst[j // HT], 16 * i)
                        nc.vector.tensor_tensor(kvj[:, j // HT, j % HT, :, :], kv[:, j, :].rearrange("p (w d) -> p w d", w=2),
                                                ps[:, j % HT, 0:D].unsqueeze(1).to_broadcast([P, 2, D]), ALU.add).then_inc(s_add, 1)
                    if 1 <= j < T + 1:
                        u = j - 1
                        dve.wait_ge(s_add, s)
                        nc.vector.tensor_tensor(prod[:, u % 4, :], kvj[:, u // HT, u % HT, 0, :], ps[:, u % HT, D:2 * D],
                                                ALU.mult).then_inc(s_prod, 1)
                    if j >= 2:
                        u = j - 2
                        dve.wait_ge(s_prod, s - 1)
                        nc.vector.tensor_reduce(g.L[:, bass.ds(s - 2, 1), :].rearrange("p o h -> p (o h)"),
                                                prod[:, u % 4, :].rearrange("p (h c) -> p h c", h=H), AX, ALU.add)
            turns(dve, NS // T, body)


def seg_max(nc, z, g, layer):
    U, NSP, R = z.U, z.NSP, z.G // 4
    with Stage(nc, f"segmax{layer}") as st:
        tb = st.sb("tb", [P, 2, 4 * P])
        X = st.sb("X", [P, H, U * P])
        F = st.sb("F", [P, H, U * P])
        tail = st.sb("tail", [P, 2, H])
        row = st.sb("row", [H, 2, P])
        crow = st.sb("crow", [H, 2, P])
        carry = st.sb("carry", [P, 2, H])
        gb = st.sb("gb", [P, 2, 4, P])
        pt = st.ps("pt", [P, 2, 4 * P])
        pr = st.ps("pr", [P, 2, 4, P])
        s_tr, s_cp, s_ld, s_x, s_c, s_tail, s_row, s_crow, s_back, s_f, s_gd, s_g2, s_sub = (
            st.sem(n) for n in ("s_tr", "s_cp", "s_ld", "s_x", "s_c", "s_tail", "s_row", "s_crow", "s_back", "s_f", "s_gd", "s_g2", "s_sub"))
        s_ls = [st.sem(f"s_ls{k}") for k in range(2)]
        s_gb = [st.sem(f"s_gb{k}") for k in range(2)]
        block = st.block()
        LG = g.LD.rearrange("s h e -> (s h) e").rearrange("(r k p) e -> r p k e", k=4, p=P)
        GG = g.GD.rearrange("s h e -> (s h) e").rearrange("(r k p) e -> r p k e", k=4, p=P)

        def rows(t, h):
            return t.rearrange("(p u) h e -> p u h e", p=P)[:, :, h, :]

        @block.sync
        def _(sp):
            for r in range(R):
                sp.wait_ge(s_cp, r + 1)
                sp.dma_start(LG[r], tb[:, r % 2, :].rearrange("p (k e) -> p k e", k=4)).then_inc(s_ls[r % 2], 16)
            for k in range(min(2, R)):
                sp.wait_ge(s_ls[k], 16 * len(range(k, R, 2)))
            for h in range(H):
                sp.dma_start(X[:, h, :].rearrange("p (u e) -> p u e", e=P), rows(g.LD, h)).then_inc(s_x, 16)
            for h in range(H):
                sp.wait_ge(s_f, h + 1)
                sp.dma_start(rows(g.GD, h), X[:, h, :].rearrange("p (u e) -> p u e", e=P)).then_inc(s_gd, 16)
            sp.wait_ge(s_gd, 16 * H)
            for r in range(R):
                if r >= 2:
                    sp.wait_ge(s_g2, r - 1)
                sp.dma_start(gb[:, r % 2, :, :], GG[r]).then_inc(s_gb[r % 2], 16)

        @block.tensor
        def _(pe):
            for r in range(R):
                if r >= 2:
                    pe.wait_ge(s_cp, r - 1)
                for k in range(4):
                    s0 = 32 * (4 * r + k)
                    ins = nc.tensor.transpose(pt[:, r % 2, k * P:(k + 1) * P],
                                              g.L[:, s0:s0 + 32, :].rearrange("p s h -> p (s h)"), g.ident[:, :])
                ins.then_inc(s_tr, 1)
            for o in range(2):
                pe.wait_ge(s_tail, o + 1)
                nc.tensor.transpose(pr[0:H, o, 0, :], tail[:, o, :], g.ident[:, :]).then_inc(s_row, 1)
                pe.wait_ge(s_crow, o + 1)
                nc.tensor.transpose(pr[:, o, 1, 0:H], crow[:, o, :], g.ident[0:H, 0:H]).then_inc(s_back, 1)
            for r in range(R):
                pe.wait_ge(s_gb[r % 2], 16 * (r // 2 + 1))
                if r >= 2:
                    pe.wait_ge(s_sub, r - 1)
                for k in range(4):
                    ins = nc.tensor.transpose(pt[:, r % 2, k * P:(k + 1) * P], gb[:, r % 2, k, :], g.ident[:, :])
                ins.then_inc(s_g2, 1)

        @block.scalar
        def _(act):
            for r in range(R):
                act.wait_ge(s_sub, r + 1)
                at = g.L[:, P * r:P * (r + 1), :]
                nc.scalar.activation(at, at, ACT.Exp, scale=C ** -0.5)

        @block.vector
        def _(dve):
            n = [0]

            def link(ins):
                n[0] += 1
                ins.then_inc(s_c, 1)
                dve.wait_ge(s_c, n[0])

            for r in range(R):
                dve.wait_ge(s_tr, r + 1)
                if r >= 2:
                    dve.wait_ge(s_ls[r % 2], 16 * (r // 2))
                nc.vector.tensor_copy(tb[:, r % 2, :], pt[:, r % 2, :]).then_inc(s_cp, 1)
            dve.wait_ge(s_x, 16 * H)
            link(nc.vector.memset(crow[:, :, :], -FAR))
            for o, (src, dst, pen) in enumerate(((X, F, g.pen_prev), (F, X, g.pen_next))):
                way = slice(None) if o == 0 else slice(None, None, -1)
                last = U * P - 1 if o == 0 else 0
                for h in range(H):
                    link(nc.vector.tensor_tensor_scan(dst[:, h, way], pen[:, way], src[:, h, way], -FAR, ALU.add, ALU.max))
                nc.vector.tensor_copy(tail[:, o, :], dst[:, :, last]).then_inc(s_tail, 1)
                dve.wait_ge(s_row, o + 1)
                link(nc.vector.tensor_tensor_scan(row[:, o, way], g.pen_row[:, o, way], pr[0:H, o, 0, way], -FAR, ALU.add, ALU.max))
                ins = nc.vector.tensor_copy(crow[:, o, 1:P] if o == 0 else crow[:, o, 0:P - 1],
                                            row[:, o, 0:P - 1] if o == 0 else row[:, o, 1:P])
                ins.then_inc(s_crow, 1)
                dve.wait_ge(s_back, o + 1)
                link(nc.vector.tensor_copy(carry[:, o, :], pr[:, o, 1, 0:H]))
                for h in range(H):
                    ins = nc.vector.tensor_tensor_scan(dst[:, h, way], pen[:, way], src[:, h, way], carry[:, o, h:h + 1],
                                                       ALU.add, ALU.max)
                    if o == 0:
                        link(ins)
                    else:
                        ins.then_inc(s_f, 1)
            for r in range(R):
                dve.wait_ge(s_g2, r + 1)
                at = g.L[:, P * r:P * (r + 1), :].rearrange("p s h -> p (s h)")
                nc.vector.tensor_tensor(at, at, pt[:, r % 2, :], ALU.subtract).then_inc(s_sub, 1)


def aggregate(nc, z, g, layer):
    T, HT, NS, A = 16, 8, z.NS, D + H
    with Stage(nc, f"agg{layer}") as st:
        vb = st.sb("vb", [P, 2, HT, D])
        w = st.sb("w", [P, 2, HT, A])
        off = st.sb("off", [P, 2, HT, P])
        oh = st.sb("oh", [P, 2, HT, P])
        ps = st.ps("ps", [P, HT, 2 * D])
        s_vb = [st.sem(f"s_vb{h}") for h in range(2)]
        s_z, s_w, s_w4, s_off, s_abs, s_oh, s_pe, s_acc = (
            st.sem(n) for n in ("s_z", "s_w", "s_w4", "s_off", "s_abs", "s_oh", "s_pe", "s_acc"))
        block = st.block()

        @block.sync
        def _(sp):
            def body(i):
                for h in range(2):
                    need(sp, s_w, 2 * (i - 1) + h + 1)
                    sp.dma_start(vb[:, h, :, :], g.vjD[bass.ds(2 * i + h, 1)].rearrange("o p t d -> (o p) t d")).then_inc(s_vb[h], 16)
            turns(sp, NS // T, body)

        @block.scalar
        def _(act):
            def body(i):
                for h in range(2):
                    need(act, s_pe, (i - 1) * T + (h + 1) * HT)
                    nc.scalar.activation(w[:, h, :, D:A], g.L[:, bass.ds(i * T + h * HT, HT), :], ACT.Copy).then_inc(s_w4, 1)
                    act.wait_ge(s_off, 2 * i + h + 1)
                    nc.scalar.activation(off[:, h, :, :], off[:, h, :, :], ACT.Abs).then_inc(s_abs, 1)
                    act.wait_ge(s_abs, 2 * i + h + 1)
                    nc.scalar.activation(oh[:, h, :, :], off[:, h, :, :], ACT.Relu, bias=g.ones[:, 0:1], scale=-1.0).then_inc(s_oh, 1)
            turns(act, NS // T, body)

        @block.gpsimd
        def _(pool):
            def body(i):
                for h in range(2):
                    need(pool, s_oh, 2 * (i - 1) + h + 1)
                    nc.gpsimd.tensor_tensor(off[:, h, :, :], g.free[:, :].unsqueeze(1).to_broadcast([P, HT, P]),
                                            g.relS[:, bass.ds(i * T + h * HT, HT)].unsqueeze(2).to_broadcast([P, HT, P]),
                                            ALU.subtract).then_inc(s_off, 1)
            turns(pool, NS // T, body)

        @block.tensor
        def _(pe):
            def body(i):
                for j in range(T):
                    s, h = i * T + j, j // HT
                    if j % HT == 0:
                        for sem in (s_w, s_w4, s_oh):
                            pe.wait_ge(sem, 2 * i + h + 1)
                    need(pe, s_acc, s - HT + 1)
                    nc.tensor.matmul(ps[:, j % HT, 0:A], oh[:, h, j % HT, :], w[:, h, j % HT, :], start=True, stop=True).then_inc(s_pe, 1)
            turns(pe, NS // T, body)

        @block.vector
        def _(dve):
            nc.vector.memset(g.acc[:, :, :], 0.0).then_inc(s_z, 1)

            def weigh(i, h):
                dve.wait_ge(s_vb[h], 16 * i + 16)
                need(dve, s_pe, (i - 1) * T + (h + 1) * HT)
                nc.vector.tensor_tensor(w[:, h, :, 0:D].rearrange("p t (h c) -> p t h c", h=H),
                                        vb[:, h, :, :].rearrange("p t (h c) -> p t h c", h=H),
                                        g.L[:, bass.ds(i * T + h * HT, HT), :].unsqueeze(3).to_broadcast([P, HT, H, C]),
                                        ALU.mult).then_inc(s_w, 1)

            def add(i, h):
                for j in range(h * HT, (h + 1) * HT):
                    s = i * T + j
                    b = dve.value_load(g.tab[0:1, bass.ds(z.NSP + s, 1)], min_val=0, max_val=z.NB - 1)
                    dve.wait_ge(s_pe, s + 1)
                    need(dve, s_acc, s)
                    at = g.acc[:, bass.ds(b, 1), :].rearrange("p o n -> p (o n)")
                    nc.vector.tensor_tensor(at, ps[:, j % HT, 0:A], at, ALU.add).then_inc(s_acc, 1)

            def body(i):
                weigh(i, 0)
                if not isinstance(i, int) or i > 0:
                    add(i - 1, 1)
                weigh(i, 1)
                add(i, 0)
            dve.wait_ge(s_z, 1)
            turns(dve, NS // T, body)
            add(NS // T - 1, 1)


def finish(nc, z, g, a):
    UB, NB = z.UB, z.NB
    with Stage(nc, "fin") as st:
        Wr = st.sb("Wr", [P, 2, EX])
        br = st.sb("br", [P, EX])
        gam = st.sb("gam", [P, D])
        bet = st.sb("bet", [P, D])
        eps = st.sb("eps", [P, 1])
        sk = st.sb("sk", [P, UB, D])
        den = st.sb("den", [P, UB, H])
        rden = st.sb("rden", [P, UB, H])
        x1 = st.sb("x1", [P, UB, D])
        stat = st.sb("stat", [P, UB, 6])
        mv = st.sb("mv", [P, 2, UB, 2])
        sd = st.sb("sd", [P, 2, UB])
        rs = st.sb("rs", [P, 2, UB])
        xa = st.sb("xa", [P, UB, D])
        xn = st.sb("xn", [P, UB, D])
        xT = st.sb("xT", [P, UB, 2, P])
        pT = st.ps("pT", [P, 2, 2 * D])
        pl = st.ps("pl", [P, 2, 2 * D])
        s_w, s_eps, s_c, s_x1, s_mv, s_sd, s_xn, s_tr, s_xT, s_pl, s_lg, s_r, s_step = (
            st.sem(n) for n in ("s_w", "s_eps", "s_c", "s_x1", "s_mv", "s_sd", "s_xn", "s_tr", "s_xT", "s_pl", "s_lg", "s_r", "s_step"))
        s_sk = [st.sem(f"s_sk{j}") for j in range(UB)]
        s_st = [st.sem(f"s_st{j}") for j in range(UB)]
        block = st.block()

        @block.sync
        def _(sp):
            sp.dma_start(Wr[:, :, :], a["Wr"].rearrange("(c p) n -> p c n", p=P)).then_inc(s_w, 16)
            for t, n in ((br, "br"), (gam, "gamma"), (bet, "beta")):
                sp.dma_start(t[:, :], a[n].partition_broadcast(P)).then_inc(s_w, 16)

            def body(i):
                for j in range(UB):
                    b = i * UB + j
                    need(sp, s_x1, b - UB + 1)
                    sp.dma_start(sk[:, j, :], g.skipD[bass.ds(b * P, P), :]).then_inc(s_sk[j], 16)
            turns(sp, NB // UB, body)

        @block.scalar
        def _(act):
            act.wait_ge(s_eps, 1)

            def body(i):
                for o in range(2):
                    act.wait_ge(s_mv, 2 * i + o + 1)
                    nc.scalar.activation(sd[:, o, :], mv[:, o, :, 1], ACT.Sqrt, bias=eps[:, 0:1]).then_inc(s_sd, 1)
                for j in range(UB):
                    b = i * UB + j
                    act.wait_ge(s_xn, b + 1)
                    act.dma_start(g.x1D[bass.ds(b * P, P), :], x1[:, j, :]).then_inc(s_st[j], 16)
                    act.dma_start(g.xnD[bass.ds(b * P, P), :], xn[:, j, :]).then_inc(s_st[j], 16)
                for j in range(UB):
                    b = i * UB + j
                    act.wait_ge(s_tr, b + 1)
                    need(act, s_pl, b - UB + 1)
                    nc.scalar.activation(xT[:, j, :, :], pT[:, j % 2, 0:D].rearrange("p (c m) -> p c m", c=2), ACT.Copy).then_inc(s_xT, 1)
            turns(act, NB // UB, body)
            for j in range(UB):
                act.wait_ge(s_st[j], 32 * (NB // UB))

        @block.tensor
        def _(pe):
            pe.wait_ge(s_w, 64)

            def body(i):
                for j in range(UB + 1):
                    if j < UB:
                        b = i * UB + j
                        pe.wait_ge(s_xn, b + 1)
                        need(pe, s_xT, b - back(j, 2, UB) + 1)
                        for c in range(2):
                            ins = nc.tensor.transpose(pT[:, j % 2, c * P:(c + 1) * P], xn[:, j, c * P:(c + 1) * P], g.ident[:, :])
                        ins.then_inc(s_tr, 1)
                    if j > 0:
                        u, b = j - 1, i * UB + j - 1
                        pe.wait_ge(s_xT, b + 1)
                        need(pe, s_lg, b - back(u, 2, UB) + 1)
                        for c in range(2):
                            ins = nc.tensor.matmul(pl[:, u % 2, 0:EX], xT[:, u, c, :], Wr[:, c, :], start=(c == 0), stop=(c == 1))
                        ins.then_inc(s_pl, 1)
            turns(pe, NB // UB, body)

        @block.vector
        def _(dve):
            nc.vector.memset(eps[:, :], EPS).then_inc(s_eps, 1)
            dve.wait_ge(s_w, 64)
            PER = 2 + 6 * UB

            def body(i):
                n = [0]

                def link(ins):
                    n[0] += 1
                    ins.then_inc(s_c, 1)

                def seen():
                    dve.wait_ge(s_c, i * PER + n[0])

                at = g.acc[:, bass.ds(i * UB, UB), :]
                link(nc.vector.tensor_scalar(den[:, :, :], at[:, :, D:D + H], 1e-16, None, ALU.add))
                seen()
                link(nc.vector.reciprocal(rden[:, :, :], den[:, :, :]))
                seen()
                for j in range(UB):
                    need(dve, s_st[j], 32 * i)
                    link(nc.vector.tensor_tensor(x1[:, j, :].rearrange("p (h c) -> p h c", h=H),
                                                 at[:, j, 0:D].rearrange("p (h c) -> p h c", h=H),
                                                 rden[:, j, :].unsqueeze(2).to_broadcast([P, H, C]), ALU.mult))
                seen()
                for j in range(UB):
                    dve.wait_ge(s_sk[j], 16 * i + 16)
                    nc.vector.tensor_tensor(x1[:, j, :], x1[:, j, :], sk[:, j, :], ALU.add).then_inc(s_x1, 1)
                dve.wait_ge(s_x1, (i + 1) * UB)
                for o, (src, dst) in enumerate(((x1, xa), (xa, xn))):
                    for j in range(UB):
                        link(nc.vector.bn_stats(stat[:, j, :], src[:, j, :]))
                    seen()
                    dve.sem_inc(s_step, 1)
                    for j in range(UB):
                        ins = nc.vector.bn_aggr(mv[:, o, j, :], stat[:, j, :])
                    ins.then_inc(s_mv, 1)
                    dve.wait_ge(s_sd, 2 * i + o + 1)
                    nc.vector.reciprocal(rs[:, o, :], sd[:, o, :]).then_inc(s_r, 1)
                    dve.wait_ge(s_r, 2 * i + o + 1)
                    for j in range(UB):
                        if o == 1:
                            need(dve, s_tr, i * UB + j - UB + 1)
                        link(nc.vector.tensor_scalar(dst[:, j, :], src[:, j, :], mv[:, o, j, 0:1], rs[:, o, j:j + 1],
                                                     ALU.subtract, ALU.mult))
                    seen()
                for j in range(UB):
                    link(nc.vector.tensor_tensor(xn[:, j, :], xn[:, j, :], gam[:, :], ALU.mult))
                seen()
                for j in range(UB):
                    nc.vector.tensor_tensor(xn[:, j, :], xn[:, j, :], bet[:, :], ALU.add).then_inc(s_xn, 1)
                for j in range(UB):
                    b = i * UB + j
                    dve.wait_ge(s_pl, b + 1)
                    nc.vector.tensor_tensor(g.lg[:, bass.ds(b, 1), :].rearrange("p o e -> p (o e)"), pl[:, j % 2, 0:EX], br[:, :],
                                            ALU.add).then_inc(s_lg, 1)
                assert n[0] == PER, n[0]
            turns(dve, NB // UB, body)


def route(nc, z, g):
    NB, NE = z.NB, z.NE
    with Stage(nc, "route") as st:
        top = st.sb("top", [P, NB, 8])
        idx = st.sb("idx", [P, NB, 8], U32)
        pick = st.sb("pick", [P, 2, NB])
        dif = st.sb("dif", [P, NB])
        ex = st.sb("ex", [P, NB])
        ex1 = st.sb("ex1", [P, NB])
        e8i = st.sb("e8i", [P, EX], I32)
        e8 = st.sb("e8", [P, EX])
        tri = st.sb("tri", [P, P])
        O = st.sb("O", [P, 2, NB, EX])
        both = st.sb("both", [P, NB, EX])
        tot = st.sb("tot", [P, NB, EX])
        inc = st.sb("inc", [P, NB, EX])
        place = st.sb("place", [P, NB, EX])
        cnt = st.sb("cnt", [P, EX])
        cnti = st.sb("cnti", [P, EX], I32)
        tl = st.sb("tl", [P, EX])
        end = st.sb("end", [P, EX])
        off = st.sb("off", [P, EX])
        tmp = st.sb("tmp", [P, NB, EX])
        posf = st.sb("posf", [P, 2, NB])
        ti = st.sb("ti", [P, NE], I32)
        tf = st.sb("tf", [P, NE])
        ge = st.sb("ge", [P, NE])
        et = st.sb("et", [P, NE])
        onesb = st.sb("onesb", [P, NB])
        zr = st.sb("zr", [P, 8 * D])
        pr = st.ps("pr", [P, 2, 2 * D])
        s_io, s_c, s_dif, s_exp, s_O, s_mm, s_z, s_zs = (
            st.sem(n) for n in ("s_io", "s_c", "s_dif", "s_exp", "s_O", "s_mm", "s_z", "s_zs"))
        block = st.block()

        @block.sync
        def _(sp):
            sp.wait_ge(s_z, 1)
            rows = g.xsD.rearrange("(t p) d -> p t d", p=P)
            parts = [(k, min(k + 8, NE)) for k in range(0, NE, 8)]
            for lo, hi in parts:
                sp.dma_start(rows[:, lo:hi, :], zr[:, 0:(hi - lo) * D].rearrange("p (t d) -> p t d", d=D)).then_inc(s_zs, 16)
            sp.wait_ge(s_zs, 16 * len(parts))

        @block.gpsimd
        def _(pool):
            nc.gpsimd.memset(zr[:, :], 0.0).then_inc(s_z, 1)
            nc.gpsimd.iota(e8i[:, :], [[1, EX]], base=0, channel_multiplier=0).then_inc(s_io, 1)
            nc.gpsimd.iota(ti[:, :], [[1, NE]], base=0, channel_multiplier=0).then_inc(s_io, 1)

        @block.scalar
        def _(act):
            act.wait_ge(s_dif, 1)
            nc.scalar.activation(ex[:, :], dif[:, :], ACT.Exp).then_inc(s_exp, 1)

        @block.tensor
        def _(pe):
            pe.wait_ge(s_O, 1)
            flat = both[:, :, :].rearrange("p b e -> p (b e)")
            nc.tensor.matmul(pr[:, 0, 0:NB * EX], tri[:, :], flat, start=True, stop=True)
            nc.tensor.matmul(pr[:, 1, 0:NB * EX], g.ones[:, :], flat, start=True, stop=True).then_inc(s_mm, 1)

        @block.vector
        def _(dve):
            n = [0]

            def link(ins):
                n[0] += 1
                ins.then_inc(s_c, 1)
                dve.wait_ge(s_c, n[0])

            link(nc.vector.tensor_scalar(tri[:, :], g.free[:, :], g.part[:, 0:1], None, ALU.is_gt))
            link(nc.vector.memset(onesb[:, :], 1.0))
            for b in range(NB):
                nc.vector.max(top[:, b, :], g.lg[:, b, :]).then_inc(s_c, 1)
            n[0] += NB
            dve.wait_ge(s_c, n[0])
            for b in range(NB):
                nc.vector.max_index(idx[:, b, :], top[:, b, :], g.lg[:, b, :]).then_inc(s_c, 1)
            n[0] += NB
            dve.wait_ge(s_c, n[0])
            nc.vector.tensor_tensor(dif[:, :], top[:, :, 1], top[:, :, 0], ALU.subtract).then_inc(s_dif, 1)
            for k in range(2):
                link(nc.vector.tensor_copy(pick[:, k, :], idx[:, :, k]))
            dve.wait_ge(s_io, 2)
            link(nc.vector.tensor_copy(e8[:, :], e8i[:, :]))
            for k in range(2):
                link(nc.vector.tensor_tensor(O[:, k, :, :], pick[:, k, :].unsqueeze(2).to_broadcast([P, NB, EX]),
                                             e8[:, :].unsqueeze(1).to_broadcast([P, NB, EX]), ALU.is_equal))
            nc.vector.tensor_tensor(both[:, :, :], O[:, 0, :, :], O[:, 1, :, :], ALU.add).then_inc(s_O, 1)
            dve.wait_ge(s_exp, 1)
            link(nc.vector.tensor_scalar(ex1[:, :], ex[:, :], 1.0, None, ALU.add))
            link(nc.vector.reciprocal(g.wt[:, 0, :], ex1[:, :]))
            link(nc.vector.tensor_tensor(g.wt[:, 1, :], ex[:, :], g.wt[:, 0, :], ALU.mult))
            dve.wait_ge(s_mm, 1)
            link(nc.vector.tensor_copy(tot[:, :, :], pr[:, 1, 0:NB * EX].rearrange("p (b e) -> p b e", e=EX)))
            for e in range(EX):
                link(nc.vector.tensor_tensor_scan(inc[:, :, e], onesb[:, :], tot[:, :, e], 0.0, ALU.mult, ALU.add))
            link(nc.vector.tensor_copy(cnt[:, :], inc[:, NB - 1, :]))
            link(nc.vector.tensor_tensor(inc[:, :, :], inc[:, :, :], tot[:, :, :], ALU.subtract))
            link(nc.vector.tensor_tensor(place[:, :, :], inc[:, :, :], pr[:, 0, 0:NB * EX].rearrange("p (b e) -> p b e", e=EX), ALU.add))
            link(nc.vector.tensor_scalar(cnti[:, :], cnt[:, :], float(P - 1), None, ALU.add))
            link(nc.vector.tensor_scalar(cnti[:, :], cnti[:, :], 7, None, ALU.arith_shift_right))
            link(nc.vector.tensor_copy(tl[:, :], cnti[:, :]))
            link(nc.vector.tensor_tensor_scan(end[:, :], g.ones[:, 0:EX], tl[:, :], 0.0, ALU.mult, ALU.add))
            link(nc.vector.tensor_tensor(off[:, :], end[:, :], tl[:, :], ALU.subtract))
            link(nc.vector.tensor_scalar(off[:, :], off[:, :], float(P), None, ALU.mult))
            link(nc.vector.tensor_tensor(place[:, :, :], place[:, :, :], off[:, :].unsqueeze(1).to_broadcast([P, NB, EX]), ALU.add))
            for k in range(2):
                link(nc.vector.tensor_tensor(tmp[:, :, :], O[:, k, :, :], place[:, :, :], ALU.mult))
                link(nc.vector.tensor_reduce(posf[:, k, :], tmp[:, :, :], AX, ALU.add))
            link(nc.vector.tensor_copy(g.pos[:, :, :].rearrange("p b k -> p k b"), posf[:, :, :]))
            link(nc.vector.tensor_copy(tf[:, :], ti[:, :]))
            link(nc.vector.memset(et[:, :], 0.0))
            for e in range(EX - 1):
                link(nc.vector.tensor_scalar(ge[:, :], tf[:, :], end[:, e:e + 1], None, ALU.is_ge))
                link(nc.vector.tensor_tensor(et[:, :], et[:, :], ge[:, :], ALU.add))
            nc.vector.tensor_copy(g.etab[:, :], et[0:1, :])


def dispatch(nc, z, g):
    UB, NB = z.UB, z.NB
    with Stage(nc, "disp") as st:
        xr = st.sb("xr", [P, UB, D])
        ix = st.sb("ix", [P, UB, 2], I32)
        s_x = [st.sem(f"s_x{j}") for j in range(UB)]
        s_sc = [st.sem(f"s_sc{j}") for j in range(UB)]
        s_ix, s_step, s_free = st.sem("s_ix"), st.sem("s_step"), st.sem("s_free")
        block = st.block()

        @block.sync
        def _(sp):
            def body(i):
                for j in range(UB):
                    need(sp, s_sc[j], 32 * i)
                    sp.dma_start(xr[:, j, :], g.xnD[bass.ds((i * UB + j) * P, P), :]).then_inc(s_x[j], 16)
            turns(sp, NB // UB, body)

        @block.gpsimd
        def _(pool):
            def body(i):
                for j in range(UB):
                    need(pool, s_sc[j], 32 * i)
                nc.gpsimd.tensor_copy(ix[:, :, :], g.pos[:, bass.ds(i * UB, UB), :]).then_inc(s_ix, 1)
                pool.wait_ge(s_ix, i + 1)
                for j in range(UB):
                    pool.wait_ge(s_x[j], 16 * i + 16)
                    pool.sem_inc(s_step, 1)
                    for k in range(2):
                        nc.gpsimd.indirect_dma_start(
                            out=g.xsD, out_offset=bass.IndirectOffsetOnAxis(ap=ix[:, j, k:k + 1].bitcast(U32), axis=0),
                            in_=xr[:, j, :], in_offset=None).then_inc(s_sc[j], 16)
            turns(pool, NB // UB, body)
            for j in range(UB):
                pool.wait_ge(s_sc[j], 32 * (NB // UB))


def experts(nc, z, g, a):
    UE, NE, KH = 6, z.NE, HID // P
    with Stage(nc, "exp") as st:
        W1 = st.sb("W1", [P, EX, 2, HID])
        W2 = st.sb("W2", [P, EX, KH, D])
        b1 = st.sb("b1", [P, EX, HID])
        b2 = st.sb("b2", [P, EX, D])
        xr = st.sb("xr", [P, UE, D])
        xT = st.sb("xT", [P, 2, D])
        hb = st.sb("hb", [P, 2, HID])
        hg = st.sb("hg", [P, 2, HID])
        hT = st.sb("hT", [P, 2, HID])
        yo = st.sb("yo", [P, UE, D])
        pX = st.ps("pX", [P, 2, 2 * D])
        pH = st.ps("pH", [P, 2, HID])
        pT = st.ps("pT", [P, 2, HID])
        pY = st.ps("pY", [P, 2, 2 * D])
        s_w, s_tx, s_xT, s_h, s_hb, s_hg, s_th, s_hT, s_y, s_yo = (
            st.sem(n) for n in ("s_w", "s_tx", "s_xT", "s_h", "s_hb", "s_hg", "s_th", "s_hT", "s_y", "s_yo"))
        s_x = [st.sem(f"s_x{j}") for j in range(UE)]
        s_st = [st.sem(f"s_st{j}") for j in range(UE)]
        block = st.block()
        n_turns = NE // UE

        def piped(eng, stages):
            deep = max(d for d, _ in stages)

            def body(i):
                for j in range(UE):
                    for d, f in stages:
                        if j >= d:
                            f(i, j - d)
                        elif not isinstance(i, int) or i > 0:
                            f(i - 1, j - d + UE)
            turns(eng, n_turns, body, peel=2)
            for j in range(deep):
                for d, f in stages:
                    if j < d:
                        f(n_turns - 1, j - d + UE)

        @block.sync
        def _(sp):
            for e in range(EX):
                sp.dma_start(W1[:, e, :, :], a["W1"][e].rearrange("(c p) n -> p c n", p=P)).then_inc(s_w, 16)
                sp.dma_start(W2[:, e, :, :], a["W2"][e].rearrange("(c p) n -> p c n", p=P)).then_inc(s_w, 16)
            sp.dma_start(b1[:, :, :].rearrange("p e n -> p (e n)"), a["b1"].rearrange("e n -> (e n)").partition_broadcast(P)).then_inc(s_w, 16)
            sp.dma_start(b2[:, :, :].rearrange("p e n -> p (e n)"), a["b2"].rearrange("e n -> (e n)").partition_broadcast(P)).then_inc(s_w, 16)

            def body(i):
                for j in range(UE):
                    t = i * UE + j
                    need(sp, s_tx, t - UE + 1)
                    sp.dma_start(xr[:, j, :], g.xsD[bass.ds(t * P, P), :]).then_inc(s_x[j], 16)
            turns(sp, n_turns, body)

        @block.tensor
        def _(pe):
            pe.wait_ge(s_w, 16 * (2 * EX + 2))

            def expert(t):
                return pe.value_load(g.etab[0:1, bass.ds(t, 1)], min_val=0, max_val=EX - 1)

            def x_transpose(i, j):
                t = i * UE + j
                pe.wait_ge(s_x[j], 16 * i + 16)
                need(pe, s_xT, t - 1)
                for c in range(2):
                    ins = nc.tensor.transpose(pX[:, j % 2, c * P:(c + 1) * P], xr[:, j, c * P:(c + 1) * P], g.ident[:, :])
                ins.then_inc(s_tx, 1)

            def first(i, j):
                t = i * UE + j
                e = expert(t)
                pe.wait_ge(s_xT, t + 1)
                need(pe, s_hb, t - 1)
                for c in range(2):
                    ins = nc.tensor.matmul(pH[:, j % 2, :], xT[:, j % 2, c * P:(c + 1) * P],
                                           W1[:, bass.ds(e, 1), c, :].rearrange("p o n -> p (o n)"), start=(c == 0), stop=(c == 1))
                ins.then_inc(s_h, 1)

            def h_transpose(i, j):
                t = i * UE + j
                pe.wait_ge(s_hg, t + 1)
                need(pe, s_hT, t - 1)
                for c in range(KH):
                    ins = nc.tensor.transpose(pT[:, j % 2, c * P:(c + 1) * P], hg[:, j % 2, c * P:(c + 1) * P], g.ident[:, :])
                ins.then_inc(s_th, 1)

            def second(i, j):
                t = i * UE + j
                e = expert(t)
                pe.wait_ge(s_hT, t + 1)
                need(pe, s_yo, t - 1)
                for c in range(KH):
                    ins = nc.tensor.matmul(pY[:, j % 2, 0:D], hT[:, j % 2, c * P:(c + 1) * P],
                                           W2[:, bass.ds(e, 1), c, :].rearrange("p o n -> p (o n)"), start=(c == 0), stop=(c == KH - 1))
                ins.then_inc(s_y, 1)
            piped(pe, ((0, x_transpose), (1, first), (2, h_transpose), (3, second)))

        @block.scalar
        def _(act):
            def x_copy(i, j):
                t = i * UE + j
                act.wait_ge(s_tx, t + 1)
                need(act, s_h, t - 1)
                nc.scalar.activation(xT[:, j % 2, :], pX[:, j % 2, 0:D], ACT.Copy).then_inc(s_xT, 1)

            def gelu(i, j):
                t = i * UE + j
                act.wait_ge(s_hb, t + 1)
                need(act, s_th, t - 1)
                nc.scalar.activation(hg[:, j % 2, :], hb[:, j % 2, :], ACT.Gelu).then_inc(s_hg, 1)

            def h_copy(i, j):
                t = i * UE + j
                act.wait_ge(s_th, t + 1)
                need(act, s_y, t - 1)
                nc.scalar.activation(hT[:, j % 2, :], pT[:, j % 2, :], ACT.Copy).then_inc(s_hT, 1)

            def store(i, j):
                act.wait_ge(s_yo, i * UE + j + 1)
                act.dma_start(g.ysD[bass.ds((i * UE + j) * P, P), :], yo[:, j, :]).then_inc(s_st[j], 16)
            piped(act, ((0, x_copy), (1, gelu), (2, h_copy), (4, store)))
            for j in range(UE):
                act.wait_ge(s_st[j], 16 * n_turns)

        @block.vector
        def _(dve):
            dve.wait_ge(s_w, 16 * (2 * EX + 2))

            def bias1(i, j):
                t = i * UE + j
                e = dve.value_load(g.etab[0:1, bass.ds(t, 1)], min_val=0, max_val=EX - 1)
                dve.wait_ge(s_h, t + 1)
                need(dve, s_hg, t - 1)
                nc.vector.tensor_tensor(hb[:, j % 2, :], pH[:, j % 2, :], b1[:, bass.ds(e, 1), :].rearrange("p o n -> p (o n)"),
                                        ALU.add).then_inc(s_hb, 1)

            def bias2(i, j):
                t = i * UE + j
                e = dve.value_load(g.etab[0:1, bass.ds(t, 1)], min_val=0, max_val=EX - 1)
                dve.wait_ge(s_y, t + 1)
                need(dve, s_st[j], 16 * i)
                nc.vector.tensor_tensor(yo[:, j, :], pY[:, j % 2, 0:D], b2[:, bass.ds(e, 1), :].rearrange("p o n -> p (o n)"),
                                        ALU.add).then_inc(s_yo, 1)
            piped(dve, ((1, bias1), (3, bias2)))


def combine(nc, z, g, out):
    UB, NB = z.UB, z.NB
    with Stage(nc, "comb") as st:
        yr = st.sb("yr", [P, UB, 2, D])
        x1 = st.sb("x1", [P, UB, D])
        xo = st.sb("xo", [P, UB, D])
        ix = st.sb("ix", [P, 2, UB, 2], I32)
        s_y = [st.sem(f"s_y{j}") for j in range(UB)]
        s_x = [st.sem(f"s_x{j}") for j in range(UB)]
        s_st = [st.sem(f"s_st{j}") for j in range(UB)]
        s_ix, s_step, s_t, s_o = (st.sem(n) for n in ("s_ix", "s_step", "s_t", "s_o"))
        block = st.block()

        @block.sync
        def _(sp):
            def body(i):
                for j in range(UB):
                    b = i * UB + j
                    need(sp, s_t, b - UB + 1)
                    sp.dma_start(x1[:, j, :], g.x1D[bass.ds(b * P, P), :]).then_inc(s_x[j], 16)
            turns(sp, NB // UB, body)

        @block.gpsimd
        def _(pool):
            def body(i):
                need(pool, s_o, (i - 1) * UB + UB)
                nc.gpsimd.tensor_copy(ix[:, 0, :, :], g.pos[:, bass.ds(i * UB, UB), :]).then_inc(s_ix, 1)
                pool.wait_ge(s_ix, i + 1)
                pool.sem_inc(s_step, 1)
                for j in range(UB):
                    for k in range(2):
                        nc.gpsimd.indirect_dma_start(
                            out=yr[:, j, k, :], out_offset=None, in_=g.ysD,
                            in_offset=bass.IndirectOffsetOnAxis(ap=ix[:, 0, j, k:k + 1].bitcast(U32), axis=0),
                        ).then_inc(s_y[j], 16)
            turns(pool, NB // UB, body)

        @block.scalar
        def _(act):
            def body(i):
                for j in range(UB):
                    b = i * UB + j
                    act.wait_ge(s_o, b + 1)
                    act.dma_start(out[bass.ds(b * P, P), :], xo[:, j, :]).then_inc(s_st[j], 16)
            turns(act, NB // UB, body)
            for j in range(UB):
                act.wait_ge(s_st[j], 16 * (NB // UB))

        @block.vector
        def _(dve):
            def body(i):
                for j in range(UB):
                    b = i * UB + j
                    dve.wait_ge(s_y[j], 32 * i + 32)
                    dve.wait_ge(s_x[j], 16 * i + 16)
                    need(dve, s_st[j], 16 * i)
                    nc.vector.scalar_tensor_tensor(out=xo[:, j, :], in0=yr[:, j, 0, :], scalar=g.wt[:, 0, bass.ds(b, 1)],
                                                   in1=x1[:, j, :], op0=ALU.mult, op1=ALU.add).then_inc(s_t, 1)
                    dve.wait_ge(s_t, b + 1)
                    nc.vector.scalar_tensor_tensor(out=xo[:, j, :], in0=yr[:, j, 1, :], scalar=g.wt[:, 1, bass.ds(b, 1)],
                                                   in1=xo[:, j, :], op0=ALU.mult, op1=ALU.add).then_inc(s_o, 1)
            turns(dve, NB // UB, body)


GNN = [w + n for n in "12" for w in ("Wq", "bq", "Wk", "bk", "Wv", "bv", "We", "Ws", "bs")]


def build(nc, z, a, out):
    g = Record()

    def dram(name, shape, dt=F32):
        return nc.dram_tensor(name, shape, dt, kind="Internal").ap()

    def keep(ctx, name, shape, dt=F32):
        return ctx.enter_context(nc.sbuf_tensor(name, shape, dt))

    NP = z.NB * P
    g.tabD = dram("tabD", (2, z.NSP), I32)
    g.relD = dram("relD", (z.NSP, P))
    g.keyD = dram("keyD", (z.NSP * P + 2,))
    g.xTD = dram("xTD", (NP, D))
    g.kvD = dram("kvD", (NP, 2 * D))
    g.baseD = dram("baseD", (NP, D))
    g.resD = dram("resD", (NP, D))
    g.skipD = dram("skipD", (NP, D))
    g.vjD = dram("vjD", (z.NS // 8, P, 8, D))
    g.LD = dram("LD", (z.NSP, H, P))
    g.GD = dram("GD", (z.NSP, H, P))
    g.x1D = dram("x1D", (NP, D))
    g.xnD = dram("xnD", (NP, D))
    g.xsD = dram("xsD", (z.NE * P, D))
    g.ysD = dram("ysD", (z.NE * P, D))
    with ExitStack() as whole:
        g.ident = keep(whole, "ident", [P, P])
        g.part = keep(whole, "part", [P, 1])
        g.free = keep(whole, "free", [P, P])
        g.ones = keep(whole, "ones", [P, P])
        g.lg = keep(whole, "lg", [P, z.NB, EX])
        g.pos = keep(whole, "pos", [P, z.NB, 2], I32)
        g.wt = keep(whole, "wt", [P, 2, z.NB])
        g.etab = keep(whole, "etab", [1, z.NE], I32)
        constants(nc, g)
        with ExitStack() as edges:
            g.tab = keep(edges, "tab", [1, 2 * z.NSP], I32)
            g.srcS = keep(edges, "srcS", [P, z.NSP], I32)
            g.relS = keep(edges, "relS", [P, z.NSP])
            g.pen_prev = keep(edges, "pen_prev", [P, z.U * P])
            g.pen_next = keep(edges, "pen_next", [P, z.U * P])
            g.pen_row = keep(edges, "pen_row", [H, 2, P])
            plan(nc, z, g, a["src_t"], a["dst_t"], a["dst_first"])
            g.acc = keep(edges, "acc", [P, z.NB, D + H])
            with Stage(nc, "mixkv") as st:
                g.kTm, g.vm = st.sb("kTm", [P, NP]), st.sb("vm", [P, NP])
                nodes(nc, z, g, 1, a)
                mix(nc, z, g, a)
            g.L = keep(edges, "L", [P, z.NSP, H])
            for layer in (1, 2):
                if layer == 2:
                    nodes(nc, z, g, 2, a)
                logits(nc, z, g, layer, a)
                seg_max(nc, z, g, layer)
                aggregate(nc, z, g, layer)
            finish(nc, z, g, a)
        route(nc, z, g)
        dispatch(nc, z, g)
        experts(nc, z, g, a)
        combine(nc, z, g, out)


def kernel(**inputs):
    import numpy as np
    import concourse.bacc as bacc
    from concourse.bass_utils import run_bass_kernel_spmd as run

    x, src, dst, ea = (np.asarray(inputs[n]) for n in ("x", "src", "dst", "edge_attr_194"))
    z = sizes(x.shape[0], src.shape[0])
    pad = z.NT * P - z.E
    lay = {
        "x": np.pad(x, ((0, z.NB * P - z.N), (0, 0))),
        "src_t": np.pad(src, (0, pad)).reshape(z.NT, P),
        "dst_t": np.pad(dst, (0, pad), constant_values=z.NB * P - 1).reshape(z.NT, P),
        "ea_t": np.ascontiguousarray(np.pad(ea, ((0, pad), (0, 0))).reshape(z.NT, P, 2, EK).transpose(0, 3, 2, 1)).reshape(z.NT, EK, 2 * P),
    }
    lay["dst_first"] = np.ascontiguousarray(lay["dst_t"][:, 0])
    for n in GNN:
        lay[n] = np.asarray(inputs["L0_gnn_" + n])
    lay["W_qkv"] = np.asarray(inputs["L0_mix_W_qkv"])
    lay["Wq_mix_T"] = np.ascontiguousarray(lay["W_qkv"][:, :MH].T)
    lay["W_out"] = np.asarray(inputs["L0_mix_W_out"])
    lay["b_out"] = np.asarray(inputs["L0_mix_b_out"])
    for n in ("gamma", "beta", "Wr", "br", "W1", "b1", "W2", "b2"):
        lay[n] = np.asarray(inputs["L0_ffn_" + n])
    nc = bacc.Bacc("TRN2", target_bir_lowering=False, num_devices=1)
    arrays, a = {}, {}
    for n, v in lay.items():
        arrays[n + "_dram"] = v
        a[n] = nc.dram_tensor(n + "_dram", v.shape, mybir.dt.from_np(v.dtype), kind="ExternalInput").ap()
    out = nc.dram_tensor("out_dram", (z.NB * P, D), F32, kind="ExternalOutput").ap()
    build(nc, z, a, out)
    return run(nc, [arrays], core_ids=[0]).results[0]["out_dram"][:z.N]
```

```python
from contextlib import ExitStack

import concourse.bass as bass
from concourse import mybir

P = 128
D = 256
H = 4
C = D // H
ED = 194
EK = ED // 2
MH = 128
MC = 32
EX = 8
HID = 512
EPS = 1e-5
FEW = 255.0
FAR = 1e30

F32 = mybir.dt.float32
I32 = mybir.dt.int32
U8 = mybir.dt.uint8
U32 = mybir.dt.uint32
ALU = mybir.AluOpType
ACT = mybir.ActivationFunctionType
AX = mybir.AxisListType.X


class Record:
    pass


def sizes(n_nodes, n_edges):
    z = Record()
    z.N, z.E = n_nodes, n_edges
    z.NB = -(-n_nodes // P)
    z.NT = -(-n_edges // P)
    z.NT += -(z.NT + z.NB - 1) % 16
    z.NS = z.NT + z.NB - 1
    z.NSP = -(-z.NS // P) * P
    z.U = z.NSP // P
    z.G = z.NSP // 32
    z.NE = -(-(2 * z.NB + EX - 1) // 6) * 6
    z.UB = max(d for d in range(1, 8) if z.NB % d == 0)
    return z


class Stage:

    def __init__(self, nc, name):
        self.nc, self.name, self.ctx, self.sems = nc, name, ExitStack(), []

    def __enter__(self):
        return self

    def __exit__(self, *a):
        self.ctx.close()
        if self.sems:
            self.nc.clear_and_free_semaphores(self.sems)
            self.nc.all_engine_barrier()

    def sb(self, name, shape, dt=F32):
        return self.ctx.enter_context(self.nc.sbuf_tensor(f"{self.name}_{name}", shape, dt))

    def ps(self, name, shape, dt=F32):
        return self.ctx.enter_context(self.nc.psum_tensor(f"{self.name}_{name}", shape, dt))

    def sem(self, name):
        self.sems.append(self.nc.alloc_semaphore(f"{self.name}_{name}"))
        return self.sems[-1]

    def block(self):
        return self.ctx.enter_context(self.nc.Block())


def table(nc, eng, entries, most):
    return nc.values_load_multi_w_load_instructions(
        entries, engines=[eng.engine], min_val=0, max_val=most,
        skip_runtime_bounds_check_because="plan() makes only tiles, blocks and experts that exist, for any dst in range")[1]


def back(j, ring, unroll):
    return ring if j >= ring else j + unroll - max(k for k in range(unroll) if k % ring == j % ring)


def constants(nc, g):
    with Stage(nc, "const") as st:
        s_iota, s_f = st.sem("s_iota"), st.sem("s_cast")
        pi = st.sb("pi", [P, 1], I32)
        fi = st.sb("fi", [P, P], I32)
        block = st.block()

        @block.gpsimd
        def _(pool):
            nc.gpsimd.iota(pi[:, :], [[0, 1]], base=0, channel_multiplier=1).then_inc(s_iota, 1)
            nc.gpsimd.iota(fi[:, :], [[1, P]], base=0, channel_multiplier=0).then_inc(s_iota, 1)

        @block.vector
        def _(dve):
            dve.wait_ge(s_iota, 2)
            nc.vector.tensor_copy(g.part[:, :], pi[:, :]).then_inc(s_f, 1)
            nc.vector.tensor_copy(g.free[:, :], fi[:, :]).then_inc(s_f, 1)
            dve.wait_ge(s_f, 2)
            nc.vector.tensor_scalar(g.ident[:, :], g.free[:, :], g.part[:, 0:1], None, ALU.is_equal)
            nc.vector.memset(g.ones[:, :], 1.0)


def plan(nc, z, g, src_t, dst_t, dst_first):
    U, NSP, NT = z.U, z.NSP, z.NT
    with Stage(nc, "plan") as st:
        first = st.sb("first", [P, NT], I32)
        fblk = st.sb("fblk", [P, NT], I32)
        iot = st.sb("iot", [P, NT], I32)
        cross = st.sb("cross", [P, NT])
        hit = st.sb("hit", [P, NT])
        sidx = st.sb("sidx", [P, U], I32)
        sval = st.sb("sval", [P, U])
        tS = st.sb("tS", [P, U])
        bS = st.sb("bS", [P, U])
        b128 = st.sb("b128", [P, U])
        tI = st.sb("tI", [P, U], I32)
        bI = st.sb("bI", [P, U], I32)
        srcR = st.sb("srcR", [P, U, P], I32)
        dstR = st.sb("dstR", [P, U, P], I32)
        srcF = st.sb("srcF", [P, U, P])
        dstF = st.sb("dstF", [P, U, P])
        rel = st.sb("rel", [P, U, P])
        relB = st.sb("relB", [P, U, P], U8)
        ok = st.sb("ok", [P, U, P])
        ok2 = st.sb("ok2", [P, U, P])
        key = st.sb("key", [P, U * P])
        kp = st.sb("kp", [P, U * P])
        kn = st.sb("kn", [P, U * P])
        edge = st.sb("edge", [1, 2])
        wp = st.sb("wp", [P, 2])
        wp4 = st.sb("wp4", [P, 2, H])
        pt = st.ps("pt", [P, 2, 4, P])
        pw = st.ps("pw", [H, 2, P])
        s_in, s_iota, s_c = st.sem("s_in"), st.sem("s_iota"), st.sem("s_c")
        s_tab, s_g, s_rel = st.sem("s_tab"), st.sem("s_g"), st.sem("s_rel")
        s_store, s_tr, s_ev, s_w, s_wt = (st.sem(n) for n in ("s_store", "s_tr", "s_ev", "s_w", "s_wt"))
        s_tst, s_tld, s_key = st.sem("s_tst"), st.sem("s_tld"), st.sem("s_key")
        NTR = 2 * U
        block = st.block()

        @block.sync
        def _(sp):
            sp.dma_start(first[:, :], dst_first.partition_broadcast(P)).then_inc(s_in, 16)
            sp.wait_ge(s_tab, 1)
            for r, tab in enumerate((tI, bI)):
                sp.dma_start(g.tabD[r, :].rearrange("(j p) -> p j", p=P), tab[:, :],
                             allow_slow_non_contiguous=True).then_inc(s_tst, 16)
            sp.wait_ge(s_tst, 32)
            sp.dma_start(g.tab[0:1, :], g.tabD.rearrange("r s -> (r s)").unsqueeze(0)).then_inc(s_tld, 16)
            sp.wait_ge(s_tld, 16)
            sp.wait_ge(s_rel, 1)
            sp.dma_start(g.relD.rearrange("(j p) e -> p j e", p=P), relB[:, :, :]).then_inc(s_store, 16)
            sp.dma_start(g.keyD[1:1 + NSP * P].rearrange("(j p e) -> p j e", p=P, e=P),
                         key[:, :].rearrange("p (j e) -> p j e", e=P)).then_inc(s_store, 16)
            sp.dma_start(g.keyD[0:1].unsqueeze(0), edge[:, 0:1]).then_inc(s_store, 16)
            sp.dma_start(g.keyD[1 + NSP * P:2 + NSP * P].unsqueeze(0), edge[:, 1:2]).then_inc(s_store, 16)
            sp.wait_ge(s_store, 64)
            for o, t in ((0, kp), (1, key), (2, kn)):
                sp.dma_start(t[:, :], g.keyD[o:o + NSP * P].rearrange("(p f) -> p f", p=P)).then_inc(s_key, 16)
            sp.wait_ge(s_key, 48)

        @block.gpsimd
        def _(pool):
            nc.gpsimd.iota(iot[:, :], [[1, NT]], base=0, channel_multiplier=0).then_inc(s_iota, 1)
            nc.gpsimd.iota(sidx[:, :], [[P, U]], base=0, channel_multiplier=1).then_inc(s_iota, 1)
            pool.wait_ge(s_tab, 1)
            for j in range(U):
                for tab, rows in ((src_t, srcR), (dst_t, dstR)):
                    nc.gpsimd.indirect_dma_start(
                        out=rows[:, j, :], out_offset=None, in_=tab,
                        in_offset=bass.IndirectOffsetOnAxis(ap=tI[:, j:j + 1].bitcast(U32), axis=0),
                    ).then_inc(s_g, 16)

        @block.vector
        def _(dve):
            n = [0]

            def link(ins):
                n[0] += 1
                ins.then_inc(s_c, 1)
                dve.wait_ge(s_c, n[0])

            dve.wait_ge(s_iota, 2)
            dve.wait_ge(s_in, 16)
            link(nc.vector.tensor_scalar(fblk[:, :], first[:, :], 7, None, ALU.arith_shift_right))
            link(nc.vector.tensor_tensor(cross[:, :], fblk[:, :], iot[:, :], ALU.add))
            link(nc.vector.tensor_copy(sval[:, :], sidx[:, :]))
            for j in range(U):
                link(nc.vector.tensor_scalar(hit[:, 1:NT], cross[:, 1:NT], sval[:, j:j + 1], None, ALU.is_le))
                link(nc.vector.tensor_reduce(tS[:, j:j + 1], hit[:, 1:NT], AX, ALU.add))
            link(nc.vector.tensor_tensor(bS[:, :], sval[:, :], tS[:, :], ALU.subtract))
            link(nc.vector.tensor_scalar(b128[:, :], bS[:, :], float(P), None, ALU.mult))
            link(nc.vector.tensor_copy(bI[:, :], bS[:, :]))
            link(nc.vector.memset(edge[:, :], -3.0))
            nc.vector.tensor_copy(tI[:, :], tS[:, :]).then_inc(s_tab, 1)
            dve.wait_ge(s_g, 32 * U)
            link(nc.vector.tensor_copy(srcF[:, :, :], srcR[:, :, :]))
            link(nc.vector.tensor_copy(dstF[:, :, :], dstR[:, :, :]))
            link(nc.vector.tensor_tensor(rel[:, :, :], dstF[:, :, :],
                                         b128[:, :].unsqueeze(2).to_broadcast([P, U, P]), ALU.subtract))
            link(nc.vector.tensor_scalar(ok[:, :, :], rel[:, :, :], 0.0, None, ALU.is_ge))
            link(nc.vector.tensor_scalar(ok2[:, :, :], rel[:, :, :], float(P), None, ALU.is_lt))
            link(nc.vector.tensor_tensor(ok[:, :, :], ok[:, :, :], ok2[:, :, :], ALU.mult))
            link(nc.vector.tensor_scalar(dstF[:, :, :], dstF[:, :, :], 2.0, None, ALU.add))
            link(nc.vector.tensor_tensor(dstF[:, :, :], dstF[:, :, :], ok[:, :, :], ALU.mult))
            link(nc.vector.tensor_scalar(key[:, :], dstF[:, :, :].rearrange("p j e -> p (j e)"), -2.0, None, ALU.add))
            link(nc.vector.tensor_scalar(rel[:, :, :], rel[:, :, :], -FEW, None, ALU.add))
            link(nc.vector.tensor_tensor(rel[:, :, :], rel[:, :, :], ok[:, :, :], ALU.mult))
            link(nc.vector.tensor_scalar(rel[:, :, :], rel[:, :, :], FEW, None, ALU.add))
            link(nc.vector.tensor_copy(relB[:, :, :], rel[:, :, :]))
            nc.vector.sem_inc(s_rel, 1)
            for i in range(NTR):
                j, dst = i % U, (g.srcS, g.relS)[i // U]
                dve.wait_ge(s_tr, i + 1)
                nc.vector.tensor_copy(dst[:, j * P:(j + 1) * P], pt[:, i % 2, 0, :]).then_inc(s_ev, 1)
            dve.wait_ge(s_key, 48)
            for o, (t, pen) in enumerate(((kp, g.pen_prev), (kn, g.pen_next))):
                link(nc.vector.tensor_tensor(t[:, :], t[:, :], key[:, :], ALU.is_equal))
                link(nc.vector.tensor_scalar(pen[:, :], t[:, :], -1.0, FAR, ALU.add, ALU.mult))
                link(nc.vector.tensor_reduce(wp[:, o:o + 1], pen[:, :], AX, ALU.min))
            link(nc.vector.tensor_copy(wp4[:, :, :], wp[:, :].unsqueeze(2).to_broadcast([P, 2, H])))
            nc.vector.sem_inc(s_w, 1)
            dve.wait_ge(s_wt, 2)
            nc.vector.tensor_copy(g.pen_row[:, :, :], pw[:, :, :])

        @block.tensor
        def _(pe):
            pe.wait_ge(s_rel, 1)
            for i in range(NTR):
                j, rows = i % U, (srcF, rel)[i // U]
                if i >= 2:
                    pe.wait_ge(s_ev, i - 1)
                nc.tensor.transpose(pt[:, i % 2, 0, :], rows[:, j, :], g.ident[:, :]).then_inc(s_tr, 1)
            pe.wait_ge(s_w, 1)
            for o in range(2):
                nc.tensor.transpose(pw[:, o, :], wp4[:, o, :], g.ident[:, :]).then_inc(s_wt, 1)


def need(eng, sem, value):
    if not isinstance(value, int) or value > 0:
        eng.wait_ge(sem, value)


def turns(eng, n, body, peel=1):
    for i in range(min(peel, n)):
        body(i)
    if n > peel:
        with eng.Fori(peel, n) as i:
            body(i)


def ahead(eng, n, body):
    body(0, n > 1)
    if n > 2:
        with eng.Fori(1, n - 1) as i:
            body(i, True)
    if n > 1:
        body(n - 1, False)


def late(i, j, lag, unroll, step):
    if j >= lag:
        step(i, j - lag)
    elif not isinstance(i, int) or i > 0:
        step(i - 1, j - lag + unroll)


def nodes(nc, z, g, layer, a):
    UB, NB, one = z.UB, z.NB, layer == 1
    with Stage(nc, f"nodes{layer}") as st:
        W = st.sb("W", [P, 2, 4 * D])
        bias = st.sb("bias", [P, 4 * D])
        eps = st.sb("eps", [P, 1])
        xin = st.sb("xin", [P, UB, D])
        res = st.sb("res", [P, UB, D])
        stat = st.sb("stat", [P, UB, 6])
        mv = st.sb("mv", [P, UB, 2])
        sd = st.sb("sd", [P, UB])
        den = st.sb("den", [P, UB, H])
        rden = st.sb("rden", [P, UB, H])
        xn = st.sb("xn", [P, UB, D])
        hs = st.sb("hs", [P, UB, D])
        xT = st.sb("xT", [P, UB, 2, P])
        kvs = st.sb("kvs", [P, UB, 3 * D])
        pj = st.ps("pj", [P, 2, 4 * D])
        pT = st.ps("pT", [P, 2, 2 * D])
        pm = st.ps("pm", [P, 2, 4, P])
        if one:
            Wm = st.sb("Wm", [P, 2, 2 * MH])
        s_w, s_eps = st.sem("s_w"), st.sem("s_eps")
        s_x = [st.sem(f"s_x{j}") for j in range(UB)]
        s_r = [st.sem(f"s_r{j}") for j in range(UB)]
        s_st = [st.sem(f"s_st{j}") for j in range(UB)]
        s_xs = [st.sem(f"s_xs{j}") for j in range(UB)]
        s_stat, s_mv, s_sd, s_rs, s_xn, s_h1, s_h2 = (st.sem(n) for n in ("s_stat", "s_mv", "s_sd", "s_rs", "s_xn", "s_h1", "s_h2"))
        s_tr, s_xT, s_pj, s_ev, s_evm = (st.sem(n) for n in ("s_tr", "s_xT", "s_pj", "s_ev", "s_evm"))
        s_sk, s_step = st.sem("s_sk"), st.sem("s_step")
        NW = 4 + 4 + (1 if one else 0)
        LAG = min(2, UB)
        J_STAT, J_DEV = min(1, UB - 1), min(3, UB - 1)
        block = st.block()

        @block.sync
        def _(sp):
            names = ["q", "k", "v", "s"]
            for n, w in enumerate(names):
                sp.dma_start(W[:, :, n * D:(n + 1) * D], a[f"W{w}{layer}"].rearrange("(c p) n -> p c n", p=P)).then_inc(s_w, 16)
                sp.dma_start(bias[:, n * D:(n + 1) * D], a[f"b{w}{layer}"].partition_broadcast(P)).then_inc(s_w, 16)
            if one:
                sp.dma_start(Wm[:, :, :], a["W_qkv"].rearrange("(c p) n -> p c n", p=P)[:, :, MH:3 * MH]).then_inc(s_w, 16)

            def body(i):
                for j in range(UB):
                    b = i * UB + j
                    need(sp, s_xn, b - UB + 1)
                    rows = bass.ds(b * P, P)
                    sp.dma_start(xin[:, j, :], (a["x"] if one else g.baseD)[rows, :]).then_inc(s_x[j], 16)
                    if not one:
                        need(sp, s_ev, b - UB + 1)
                        sp.dma_start(res[:, j, :], g.resD[rows, :]).then_inc(s_r[j], 16)
            turns(sp, NB // UB, body)

        @block.scalar
        def _(act):
            act.wait_ge(s_eps, 1)

            def store(i, j):
                b = i * UB + j
                act.wait_ge(s_ev, b + 1)
                act.dma_start(g.kvD[bass.ds(b * P, P), :], kvs[:, j, 0:2 * D]).then_inc(s_st[j], 16)
                act.dma_start((g.baseD if one else g.skipD)[bass.ds(b * P, P), :],
                              kvs[:, j, 2 * D:3 * D]).then_inc(s_st[j], 16)

            def deviation(i):
                act.wait_ge(s_mv, i + 1)
                nc.scalar.activation(sd[:, :], mv[:, :, 1], ACT.Sqrt, bias=eps[:, 0:1]).then_inc(s_sd, 1)

            def relu(i, j):
                b = i * UB + j
                act.wait_ge(s_h2, b + 1)
                need(act, s_tr, b - UB + 1)
                nc.scalar.activation(xn[:, j, :], hs[:, j, :], ACT.Relu).then_inc(s_xn, 1)

            def keep_mix(i, j):
                b = i * UB + j
                act.wait_ge(s_pj, b + 1)
                nc.scalar.activation(g.kTm[:, bass.ds(b * P, P)], pm[:, j % 2, 0, :], ACT.Copy)
                nc.scalar.activation(g.vm[:, bass.ds(b * P, P)], pm[:, j % 2, 1, :], ACT.Copy).then_inc(s_evm, 1)

            def body(i, more):
                for j in range(UB):
                    b = i * UB + j
                    act.wait_ge(s_tr, b + 1)
                    need(act, s_pj, b - UB + 1)
                    if one:
                        need(act, s_xs[j], 16 * i)
                    nc.scalar.activation(xT[:, j, :, :], pT[:, j % 2, 0:D].rearrange("p (c m) -> p c m", c=2), ACT.Copy).then_inc(s_xT, 1)
                    if one:
                        if more and j == J_DEV:
                            deviation(i + 1)
                        late(i, j, 1, UB, keep_mix)
                    elif more and j >= 2:
                        relu(i + 1, j - 2)
                    late(i, j, LAG, UB, store)
                    if one:
                        act.wait_ge(s_xT, b + 1)
                        act.dma_start(g.xTD[bass.ds(b * P, P), :], xT[:, j, :, :].rearrange("p c m -> p (c m)")).then_inc(s_xs[j], 16)
                if more and not one:
                    for j in range(max(UB - 2, 0), UB):
                        relu(i + 1, j)
            if one:
                deviation(0)
            else:
                for j in range(UB):
                    relu(0, j)
            ahead(act, NB // UB, body)
            if one:
                keep_mix(NB // UB - 1, UB - 1)
            for j in range(UB - LAG, UB):
                store(NB // UB - 1, j)
            for j in range(UB):
                act.wait_ge(s_st[j], 32 * (NB // UB))
                if one:
                    act.wait_ge(s_xs[j], 16 * (NB // UB))

        @block.tensor
        def _(pe):
            pe.wait_ge(s_w, 16 * NW)

            def transpose(i, j):
                b = i * UB + j
                pe.wait_ge(s_xn, b + 1)
                need(pe, s_xT, b - back(j, 2, UB) + 1)
                for c in range(2):
                    ins = nc.tensor.transpose(pT[:, j % 2, c * P:(c + 1) * P], xn[:, j, c * P:(c + 1) * P], g.ident[:, :])
                ins.then_inc(s_tr, 1)

            def body(i):
                transpose(i, 0)
                for j in range(UB):
                    b = i * UB + j
                    if j + 1 < UB:
                        transpose(i, j + 1)
                    pe.wait_ge(s_xT, b + 1)
                    need(pe, s_ev, b - back(j, 2, UB) + 1)
                    if one:
                        need(pe, s_evm, b - back(j, 2, UB) + 1)
                        for n in range(2):
                            for c in range(2):
                                l, r = Wm[:, c, n * MH:(n + 1) * MH], xT[:, j, c, :]
                                if n == 1:
                                    l, r = r, l
                                nc.tensor.matmul(pm[:, j % 2, n, :], l, r, start=(c == 0), stop=(c == 1))
                    for n in range(2):
                        for c in range(2):
                            ins = nc.tensor.matmul(pj[:, j % 2, n * 2 * D:(n + 1) * 2 * D], xT[:, j, c, :],
                                                   W[:, c, n * 2 * D:(n + 1) * 2 * D], start=(c == 0), stop=(c == 1))
                    ins.then_inc(s_pj, 1)
            turns(pe, NB // UB, body)

        @block.vector
        def _(dve):
            nc.vector.memset(eps[:, :], EPS).then_inc(s_eps, 1)
            dve.wait_ge(s_w, 16 * NW)

            def statistics(i):
                for j in range(UB):
                    dve.wait_ge(s_x[j], 16 * i + 16)
                    nc.vector.bn_stats(stat[:, j, :], xin[:, j, :]).then_inc(s_stat, 1)
                dve.wait_ge(s_stat, (i + 1) * UB)
                dve.sem_inc(s_step, 1)
                for j in range(UB):
                    ins = nc.vector.bn_aggr(mv[:, j, :], stat[:, j, :])
                ins.then_inc(s_mv, 1)

            def inverse(i):
                dve.wait_ge(s_sd, i + 1)
                nc.vector.reciprocal(sd[:, :], sd[:, :]).then_inc(s_rs, 1)
                dve.wait_ge(s_rs, i + 1)

            def normed(i, j):
                need(dve, s_tr, i * UB + j - UB + 1)
                nc.vector.tensor_scalar(xn[:, j, :], xin[:, j, :], mv[:, j, 0:1], sd[:, j:j + 1],
                                        ALU.subtract, ALU.mult).then_inc(s_xn, 1)

            def denominators(i):
                nc.vector.tensor_scalar(den[:, :, :], g.acc[:, bass.ds(i * UB, UB), D:D + H], 1e-16, None, ALU.add).then_inc(s_stat, 1)
                dve.wait_ge(s_stat, i + 1)
                nc.vector.reciprocal(rden[:, :, :], den[:, :, :]).then_inc(s_rs, 1)
                dve.wait_ge(s_rs, i + 1)

            def divided(i, j):
                need(dve, s_xn, i * UB + j - UB + 1)
                nc.vector.tensor_tensor(hs[:, j, :].rearrange("p (h c) -> p h c", h=H),
                                        g.acc[:, bass.ds(i * UB + j, 1), 0:D].rearrange("p o (h c) -> p (o h) c", h=H),
                                        rden[:, j, :].unsqueeze(2).to_broadcast([P, H, C]), ALU.mult).then_inc(s_h1, 1)

            def with_skip(i, j):
                dve.wait_ge(s_h1, i * UB + j + 1)
                dve.wait_ge(s_x[j], 16 * i + 16)
                nc.vector.tensor_tensor(hs[:, j, :], hs[:, j, :], xin[:, j, :], ALU.add).then_inc(s_h2, 1)

            def prepare(i, j):
                if one:
                    if j == J_STAT:
                        statistics(i)
                    if j == J_DEV:
                        inverse(i)
                    for k in range(0 if j == J_DEV else j, j + 1 if j >= J_DEV else 0):
                        normed(i, k)
                else:
                    if j == 0:
                        denominators(i)
                    divided(i, j)
                    if j > 0:
                        with_skip(i, j - 1)
                    if j == UB - 1:
                        with_skip(i, j)

            def body(i, more):
                for j in range(UB):
                    b = i * UB + j
                    dve.wait_ge(s_pj, b + 1)
                    q = g.acc[:, bass.ds(b, 1), 0:D].rearrange("p o d -> p (o d)")
                    nc.vector.tensor_tensor(q, pj[:, j % 2, 0:D], bias[:, 0:D], ALU.add)
                    need(dve, s_st[j], 32 * i)
                    ins = nc.vector.tensor_tensor(kvs[:, j, :], pj[:, j % 2, D:4 * D], bias[:, D:4 * D], ALU.add)
                    if one:
                        ins.then_inc(s_ev, 1)
                    else:
                        ins.then_inc(s_sk, 1)
                        dve.wait_ge(s_sk, b + 1)
                        dve.wait_ge(s_r[j], 16 * i + 16)
                        nc.vector.tensor_tensor(kvs[:, j, 2 * D:3 * D], kvs[:, j, 2 * D:3 * D], res[:, j, :], ALU.add).then_inc(s_ev, 1)
                    if more:
                        prepare(i + 1, j)
            for j in range(UB):
                prepare(0, j)
            ahead(dve, NB // UB, body)


def mix(nc, z, g, a):
    UB, NB, N = z.UB, z.NB, z.N
    with Stage(nc, "mix") as st:
        eb = st.sb("eb", [P, UB, P])
        ek = st.sb("ek", [P, UB, P])
        zr = st.sb("zr", [P, 4 * D])
        zero = st.sb("zero", [P, P])
        nmax = st.sb("nmax", [P, 1])
        es = st.sb("es", [P, NB])
        esum = st.sb("esum", [P, 1])
        rsum = st.sb("rsum", [P, 1])
        mask = st.sb("mask", [P, P])
        hrow = st.sb("hrow", [P, 2], I32)
        hcol = st.sb("hcol", [P, P], I32)
        rowf = st.sb("rowf", [P, 1])
        colf = st.sb("colf", [P, P])
        ctxm = st.sb("ctxm", [P, P])
        ctxT = st.sb("ctxT", [P, P])
        Wout = st.sb("Wout", [P, D])
        WqT = st.sb("WqT", [P, D])
        G = st.sb("G", [P, D])
        M = st.sb("M", [P, 2, D])
        bout = st.sb("bout", [P, D])
        xT = st.sb("xT", [P, UB, 2 * P])
        xin = st.sb("xin", [P, UB, D])
        xo = st.sb("xo", [P, UB, D])
        pe_ = st.ps("pe_", [P, 2, 4, P])
        pc = st.ps("pc", [P, 4, P])
        pg = st.ps("pg", [P, 3, 2 * D])
        po = st.ps("po", [P, 2, 2 * D])
        s_z, s_nm, s_eb, s_tr, s_ek, s_ctx, s_io, s_c, s_cm, s_ct, s_ctT, s_G, s_Gs, s_M, s_Ms, s_po, s_xo, s_w = (
            st.sem(n) for n in ("s_z", "s_nm", "s_eb", "s_tr", "s_ek", "s_ctx", "s_io", "s_c", "s_cm", "s_ct", "s_ctT",
                                "s_G", "s_Gs", "s_M", "s_Ms", "s_po", "s_xo", "s_w"))
        s_zr, s_zs = st.sem("s_zr"), st.sem("s_zs")
        s_x = [st.sem(f"s_x{j}") for j in range(UB)]
        s_st = [st.sem(f"s_st{j}") for j in range(UB)]
        block = st.block()

        @block.sync
        def _(sp):
            sp.dma_start(Wout[:, :], a["W_out"]).then_inc(s_w, 16)
            sp.dma_start(WqT[:, :], a["Wq_mix_T"]).then_inc(s_w, 16)
            sp.dma_start(bout[:, :], a["b_out"].partition_broadcast(P)).then_inc(s_w, 16)

            def body(i):
                for j in range(UB):
                    b = i * UB + j
                    rows = bass.ds(b * P, P)
                    need(sp, s_po, b - UB + 1)
                    need(sp, s_xo, b - UB + 1)
                    sp.dma_start(xT[:, j, :], g.xTD[rows, :]).then_inc(s_x[j], 16)
                    sp.dma_start(xin[:, j, :], a["x"][rows, :]).then_inc(s_x[j], 16)
            turns(sp, NB // UB, body)

        @block.gpsimd
        def _(pool):
            nc.gpsimd.iota(hrow[:, :], [[0, 2]], base=0, channel_multiplier=1).then_inc(s_io, 1)
            nc.gpsimd.iota(hcol[:, :], [[1, P]], base=0, channel_multiplier=0).then_inc(s_io, 1)
            nc.gpsimd.memset(zr[:, :], 0.0).then_inc(s_zr, 1)
            pool.wait_ge(s_zr, 1)
            rows = g.xsD.rearrange("(t p) d -> p t d", p=P)
            parts = [(k, min(k + 4, z.NE)) for k in range(0, z.NE, 4)]
            for lo, hi in parts:
                pool.dma_start(rows[:, lo:hi, :], zr[:, 0:(hi - lo) * D].rearrange("p (t d) -> p t d", d=D)).then_inc(s_zs, 16)
            pool.wait_ge(s_zs, 16 * len(parts))

        @block.scalar
        def _(act):
            act.wait_ge(s_nm, 1)

            def body(i):
                for j in range(UB):
                    b = i * UB + j
                    need(act, s_tr, b - UB + 1)
                    nc.scalar.activation(eb[:, j, :], g.kTm[:, bass.ds(b * P, P)], ACT.Exp, bias=nmax[:, 0:1],
                                         accum_out=es[:, bass.ds(b, 1)]).then_inc(s_eb, 1)
            turns(act, NB // UB, body)

            def out(i):
                for j in range(UB):
                    b = i * UB + j
                    act.wait_ge(s_xo, b + 1)
                    act.dma_start(g.resD[bass.ds(b * P, P), :], xo[:, j, :]).then_inc(s_st[j], 16)
            turns(act, NB // UB, out)
            for j in range(UB):
                act.wait_ge(s_st[j], 16 * (NB // UB))

        @block.tensor
        def _(pe):
            pe.wait_ge(s_z, 1)
            nc.tensor.matmul(pc[:, 0, :], zero[:, :], zero[:, :], start=True, stop=False)

            def body(i):
                for j in range(UB + 1):
                    if j < UB:
                        b = i * UB + j
                        pe.wait_ge(s_eb, b + 1)
                        need(pe, s_ek, b - back(j, 2, UB) + 1)
                        nc.tensor.transpose(pe_[:, j % 2, 0, :], eb[:, j, :], g.ident[:, :]).then_inc(s_tr, 1)
                    if j > 0:
                        b = i * UB + j - 1
                        pe.wait_ge(s_ek, b + 1)
                        nc.tensor.matmul(pc[:, 0, :], ek[:, j - 1, :], g.vm[:, bass.ds(b * P, P)],
                                         start=False, stop=False).then_inc(s_ctx, 1)
            turns(pe, NB // UB, body)
            nc.tensor.matmul(pc[:, 0, :], zero[:, :], zero[:, :], start=False, stop=True).then_inc(s_ctx, 1)
            pe.wait_ge(s_cm, 1)
            nc.tensor.transpose(pc[:, 1, :], ctxm[:, :], g.ident[:, :]).then_inc(s_ct, 1)
            pe.wait_ge(s_ctT, 1)
            pe.wait_ge(s_w, 48)
            nc.tensor.matmul(pg[:, 0, 0:D], ctxT[:, :], Wout[:, :], start=True, stop=True).then_inc(s_G, 1)
            pe.wait_ge(s_Gs, 1)
            for c in range(2):
                nc.tensor.matmul(pg[:, 1 + c, 0:D], WqT[:, c * P:(c + 1) * P], G[:, :], start=True, stop=True).then_inc(s_M, 1)
            pe.wait_ge(s_Ms, 1)

            def out(i):
                for j in range(UB):
                    b = i * UB + j
                    pe.wait_ge(s_x[j], 32 * i + 32)
                    need(pe, s_xo, b - back(j, 2, UB) + 1)
                    for c in range(2):
                        ins = nc.tensor.matmul(po[:, j % 2, 0:D], xT[:, j, c * P:(c + 1) * P], M[:, c, :],
                                               start=(c == 0), stop=(c == 1))
                    ins.then_inc(s_po, 1)
            turns(pe, NB // UB, out)

        @block.vector
        def _(dve):
            nc.vector.memset(zero[:, :], 0.0).then_inc(s_z, 1)
            if N < NB * P:
                nc.vector.memset(g.kTm[:, N:NB * P], -FAR)
            nc.vector.tensor_reduce(nmax[:, :], g.kTm[:, 0:N], AX, ALU.max, negate=True).then_inc(s_nm, 1)
            n = [0]

            def link(ins):
                n[0] += 1
                ins.then_inc(s_c, 1)
                dve.wait_ge(s_c, n[0])

            dve.wait_ge(s_io, 2)
            link(nc.vector.tensor_scalar(hrow[:, :], hrow[:, :], 5, None, ALU.arith_shift_right))
            link(nc.vector.tensor_scalar(hcol[:, :], hcol[:, :], 5, None, ALU.arith_shift_right))
            link(nc.vector.tensor_copy(rowf[:, :], hrow[:, 0:1]))
            link(nc.vector.tensor_copy(colf[:, :], hcol[:, :]))
            link(nc.vector.tensor_scalar(mask[:, :], colf[:, :], rowf[:, 0:1], MC ** -0.5, ALU.is_equal, ALU.mult))

            def body(i):
                for j in range(UB):
                    b = i * UB + j
                    dve.wait_ge(s_tr, b + 1)
                    need(dve, s_ctx, b - UB + 1)
                    nc.vector.tensor_copy(ek[:, j, :], pe_[:, j % 2, 0, :]).then_inc(s_ek, 1)
            turns(dve, NB // UB, body)
            dve.wait_ge(s_ctx, NB + 1)
            dve.wait_ge(s_eb, NB)
            link(nc.vector.tensor_reduce(esum[:, :], es[:, :], AX, ALU.add))
            link(nc.vector.reciprocal(rsum[:, :], esum[:, :]))
            nc.vector.scalar_tensor_tensor(out=ctxm[:, :], in0=pc[:, 0, :], scalar=rsum[:, 0:1], in1=mask[:, :],
                                           op0=ALU.mult, op1=ALU.mult).then_inc(s_cm, 1)
            dve.wait_ge(s_ct, 1)
            nc.vector.tensor_copy(ctxT[:, :], pc[:, 1, :]).then_inc(s_ctT, 1)
            dve.wait_ge(s_G, 1)
            nc.vector.tensor_copy(G[:, :], pg[:, 0, 0:D]).then_inc(s_Gs, 1)
            dve.wait_ge(s_M, 2)
            nc.vector.tensor_copy(M[:, :, :], pg[:, 1:3, 0:D]).then_inc(s_Ms, 1)
            dve.wait_ge(s_w, 48)

            def out(i):
                for j in range(UB):
                    b = i * UB + j
                    dve.wait_ge(s_x[j], 32 * i + 32)
                    need(dve, s_st[j], 16 * i)
                    link_x = nc.vector.tensor_tensor(xo[:, j, :], xin[:, j, :], bout[:, :], ALU.add)
                    link_x.then_inc(s_z, 1)
                for j in range(UB):
                    b = i * UB + j
                    dve.wait_ge(s_z, b + 2)
                    dve.wait_ge(s_po, b + 1)
                    nc.vector.tensor_tensor(xo[:, j, :], po[:, j % 2, 0:D], xo[:, j, :], ALU.add).then_inc(s_xo, 1)
            turns(dve, NB // UB, out)


def logits(nc, z, g, layer, a):
    T, HT = 16, 8
    NS = z.NS
    with Stage(nc, f"logits{layer}") as st:
        We = st.sb("We", [EK, 2, D])
        ea = st.sb("ea", [EK, T, 2, P])
        kb = st.sb("kb", [P, 2, HT * P], U8)
        far = st.sb("far", [P, HT * P])
        npart = st.sb("npart", [P, 1])
        oht = st.sb("oht", [P, 2, HT * P])
        ix = st.sb("ix", [P, 2, HT], I32)
        kv = st.sb("kv", [P, T, 2 * D])
        kvj = st.sb("kvj", [P, 2, HT, 2, D])
        prod = st.sb("prod", [P, 4, D])
        ps = st.ps("ps", [P, HT, 2 * D])
        s_ea = [st.sem(f"s_ea{j}") for j in range(T)]
        s_kv = [st.sem(f"s_kv{j}") for j in range(T)]
        s_kb = [st.sem(f"s_kb{h}") for h in range(2)]
        s_vst = [st.sem(f"s_vst{h}") for h in range(2)]
        s_spare = st.sem("s_spare")
        s_we, s_far, s_oht, s_ix, s_step, s_pe, s_add, s_prod, s_np = (
            st.sem(n) for n in ("s_we", "s_far", "s_oht", "s_ix", "s_step", "s_pe", "s_add", "s_prod", "s_np"))
        block = st.block()

        @block.sync
        def _(sp):
            sp.dma_start(We[:, :, :], a[f"We{layer}"].rearrange("(c p) n -> p c n", p=EK)).then_inc(s_we, 16)

            def body(i):
                for j in range(T):
                    s, h = i * T + j, j // HT
                    if j % HT == 0:
                        tiles = table(nc, sp, g.tab[0:1, bass.ds(s, HT)], z.NT - 1)
                        need(sp, s_far, 2 * (i - 1) + h + 1)
                        sp.sem_inc(s_spare, 1)
                        sp.dma_start(kb[:, h, :], g.relD[bass.ds(i * T + j, HT), :].rearrange("s e -> (s e)").partition_broadcast(P)).then_inc(s_kb[h], 16)
                    need(sp, s_pe, s - T + 1)
                    sp.dma_start(ea[:, j, :, :].rearrange("p c e -> p (c e)"),
                                 a["ea_t"][bass.ds(tiles[j % HT], 1), :, :].rearrange("o p n -> (o p) n")).then_inc(s_ea[j], 16)
            turns(sp, NS // T, body)

        @block.gpsimd
        def _(pool):
            if z.NSP > NS:
                nc.gpsimd.memset(g.L[:, NS:z.NSP, :], 0.0)

            def body(i):
                for h in range(2):
                    need(pool, s_add, (i - 1) * T + (h + 1) * HT)
                    nc.gpsimd.tensor_copy(ix[:, h, :], g.srcS[:, bass.ds(i * T + h * HT, HT)]).then_inc(s_ix, 1)
                    pool.wait_ge(s_ix, 2 * i + h + 1)
                    pool.sem_inc(s_step, 1)
                    for j in range(h * HT, (h + 1) * HT):
                        nc.gpsimd.indirect_dma_start(
                            out=kv[:, j, :], out_offset=None, in_=g.kvD,
                            in_offset=bass.IndirectOffsetOnAxis(ap=ix[:, h, j % HT:j % HT + 1].bitcast(U32), axis=0),
                        ).then_inc(s_kv[j], 16)
            turns(pool, NS // T, body)

        @block.scalar
        def _(act):
            act.wait_ge(s_np, 1)

            def onehot(i, h):
                act.wait_ge(s_kb[h], 16 * i + 16)
                need(act, s_oht, 2 * i + h)
                nc.scalar.activation(far[:, :], kb[:, h, :], ACT.Abs, bias=npart[:, 0:1]).then_inc(s_far, 1)
                act.wait_ge(s_far, 2 * i + h + 1)
                need(act, s_pe, (i - 1) * T + (h + 1) * HT)
                nc.scalar.activation(oht[:, h, :], far[:, :], ACT.Relu, bias=g.ones[:, 0:1], scale=-1.0).then_inc(s_oht, 1)

            def store(i, h):
                act.wait_ge(s_add, i * T + (h + 1) * HT)
                act.dma_start(g.vjD[bass.ds(2 * i + h, 1)].rearrange("o p t d -> (o p) t d"),
                              kvj[:, h, :, 1, :]).then_inc(s_vst[h], 16)

            def body(i):
                onehot(i, 0)
                if not isinstance(i, int) or i > 0:
                    store(i - 1, 1)
                onehot(i, 1)
                store(i, 0)
            turns(act, NS // T, body)
            store(NS // T - 1, 1)
            for h in range(2):
                act.wait_ge(s_vst[h], 16 * (NS // T))

        @block.tensor
        def _(pe):
            pe.wait_ge(s_we, 16)

            def body(i):
                for j in range(T):
                    s = i * T + j
                    if j % HT == 0:
                        blocks = table(nc, pe, g.tab[0:1, bass.ds(z.NSP + s, HT)], z.NB - 1)
                    pe.wait_ge(s_ea[j], 16 * i + 16)
                    need(pe, s_prod, s - HT + 1)
                    for c in range(2):
                        nc.tensor.matmul(ps[:, j % HT, 0:D], ea[:, j, c, :], We[:, c, :], start=(c == 0), stop=(c == 1))
                    if j % HT == 0:
                        pe.wait_ge(s_oht, 2 * i + j // HT + 1)
                    nc.tensor.matmul(ps[:, j % HT, D:2 * D], oht[:, j // HT, (j % HT) * P:(j % HT + 1) * P],
                                     g.acc[:, bass.ds(blocks[j % HT], 1), 0:D].rearrange("p o d -> p (o d)"), start=True, stop=True).then_inc(s_pe, 1)
            turns(pe, NS // T, body)

        @block.vector
        def _(dve):
            nc.vector.tensor_scalar(npart[:, :], g.part[:, :], -1.0, None, ALU.mult).then_inc(s_np, 1)

            def body(i):
                for j in range(T + 2):
                    s = i * T + j
                    if j < T:
                        dve.wait_ge(s_kv[j], 16 * i + 16)
                        dve.wait_ge(s_pe, s + 1)
                        if j % HT == 0:
                            need(dve, s_vst[j // HT], 16 * i)
                        nc.vector.tensor_tensor(kvj[:, j // HT, j % HT, :, :], kv[:, j, :].rearrange("p (w d) -> p w d", w=2),
                                                ps[:, j % HT, 0:D].unsqueeze(1).to_broadcast([P, 2, D]), ALU.add).then_inc(s_add, 1)
                    if 1 <= j < T + 1:
                        u = j - 1
                        dve.wait_ge(s_add, s)
                        nc.vector.tensor_tensor(prod[:, u % 4, :], kvj[:, u // HT, u % HT, 0, :], ps[:, u % HT, D:2 * D],
                                                ALU.mult).then_inc(s_prod, 1)
                    if j >= 2:
                        u = j - 2
                        dve.wait_ge(s_prod, s - 1)
                        nc.vector.tensor_reduce(g.L[:, bass.ds(s - 2, 1), :].rearrange("p o h -> p (o h)"),
                                                prod[:, u % 4, :].rearrange("p (h c) -> p h c", h=H), AX, ALU.add)
            turns(dve, NS // T, body)


def seg_max(nc, z, g, layer):
    U, NSP, R = z.U, z.NSP, z.G // 4
    with Stage(nc, f"segmax{layer}") as st:
        tb = st.sb("tb", [P, 2, 4 * P])
        X = st.sb("X", [P, H, U * P])
        F = st.sb("F", [P, H, U * P])
        tail = st.sb("tail", [P, 2, H])
        row = st.sb("row", [H, 2, P])
        crow = st.sb("crow", [H, 2, P])
        carry = st.sb("carry", [P, 2, H])
        gb = st.sb("gb", [P, 2, 4, P])
        pt = st.ps("pt", [P, 2, 4 * P])
        pr = st.ps("pr", [P, 2, 4, P])
        s_tr, s_cp, s_ld, s_x, s_c, s_tail, s_row, s_crow, s_back, s_f, s_gd, s_g2, s_sub = (
            st.sem(n) for n in ("s_tr", "s_cp", "s_ld", "s_x", "s_c", "s_tail", "s_row", "s_crow", "s_back", "s_f", "s_gd", "s_g2", "s_sub"))
        s_ls = [st.sem(f"s_ls{k}") for k in range(2)]
        s_gb = [st.sem(f"s_gb{k}") for k in range(2)]
        block = st.block()
        LG = g.LD.rearrange("s h e -> (s h) e").rearrange("(r k p) e -> r p k e", k=4, p=P)
        GG = g.GD.rearrange("s h e -> (s h) e").rearrange("(r k p) e -> r p k e", k=4, p=P)

        def rows(t, h):
            return t.rearrange("(p u) h e -> p u h e", p=P)[:, :, h, :]

        @block.sync
        def _(sp):
            for r in range(R):
                sp.wait_ge(s_cp, r + 1)
                sp.dma_start(LG[r], tb[:, r % 2, :].rearrange("p (k e) -> p k e", k=4)).then_inc(s_ls[r % 2], 16)
            for k in range(min(2, R)):
                sp.wait_ge(s_ls[k], 16 * len(range(k, R, 2)))
            for h in range(H):
                sp.dma_start(X[:, h, :].rearrange("p (u e) -> p u e", e=P), rows(g.LD, h)).then_inc(s_x, 16)
            for h in range(H):
                sp.wait_ge(s_f, h + 1)
                sp.dma_start(rows(g.GD, h), X[:, h, :].rearrange("p (u e) -> p u e", e=P)).then_inc(s_gd, 16)
            sp.wait_ge(s_gd, 16 * H)
            for r in range(R):
                if r >= 2:
                    sp.wait_ge(s_g2, r - 1)
                sp.dma_start(gb[:, r % 2, :, :], GG[r]).then_inc(s_gb[r % 2], 16)

        @block.tensor
        def _(pe):
            for r in range(R):
                if r >= 2:
                    pe.wait_ge(s_cp, r - 1)
                for k in range(4):
                    s0 = 32 * (4 * r + k)
                    ins = nc.tensor.transpose(pt[:, r % 2, k * P:(k + 1) * P],
                                              g.L[:, s0:s0 + 32, :].rearrange("p s h -> p (s h)"), g.ident[:, :])
                ins.then_inc(s_tr, 1)
            for o in range(2):
                pe.wait_ge(s_tail, o + 1)
                nc.tensor.transpose(pr[0:H, o, 0, :], tail[:, o, :], g.ident[:, :]).then_inc(s_row, 1)
                pe.wait_ge(s_crow, o + 1)
                nc.tensor.transpose(pr[:, o, 1, 0:H], crow[:, o, :], g.ident[0:H, 0:H]).then_inc(s_back, 1)
            for r in range(R):
                pe.wait_ge(s_gb[r % 2], 16 * (r // 2 + 1))
                if r >= 2:
                    pe.wait_ge(s_sub, r - 1)
                for k in range(4):
                    ins = nc.tensor.transpose(pt[:, r % 2, k * P:(k + 1) * P], gb[:, r % 2, k, :], g.ident[:, :])
                ins.then_inc(s_g2, 1)

        @block.scalar
        def _(act):
            for r in range(R):
                act.wait_ge(s_sub, r + 1)
                at = g.L[:, P * r:P * (r + 1), :]
                nc.scalar.activation(at, at, ACT.Exp, scale=C ** -0.5)

        @block.vector
        def _(dve):
            n = [0]

            def link(ins):
                n[0] += 1
                ins.then_inc(s_c, 1)
                dve.wait_ge(s_c, n[0])

            for r in range(R):
                dve.wait_ge(s_tr, r + 1)
                if r >= 2:
                    dve.wait_ge(s_ls[r % 2], 16 * (r // 2))
                nc.vector.tensor_copy(tb[:, r % 2, :], pt[:, r % 2, :]).then_inc(s_cp, 1)
            dve.wait_ge(s_x, 16 * H)
            link(nc.vector.memset(crow[:, :, :], -FAR))
            for o, (src, dst, pen) in enumerate(((X, F, g.pen_prev), (F, X, g.pen_next))):
                way = slice(None) if o == 0 else slice(None, None, -1)
                last = U * P - 1 if o == 0 else 0
                for h in range(H):
                    link(nc.vector.tensor_tensor_scan(dst[:, h, way], pen[:, way], src[:, h, way], -FAR, ALU.add, ALU.max))
                nc.vector.tensor_copy(tail[:, o, :], dst[:, :, last]).then_inc(s_tail, 1)
                dve.wait_ge(s_row, o + 1)
                link(nc.vector.tensor_tensor_scan(row[:, o, way], g.pen_row[:, o, way], pr[0:H, o, 0, way], -FAR, ALU.add, ALU.max))
                ins = nc.vector.tensor_copy(crow[:, o, 1:P] if o == 0 else crow[:, o, 0:P - 1],
                                            row[:, o, 0:P - 1] if o == 0 else row[:, o, 1:P])
                ins.then_inc(s_crow, 1)
                dve.wait_ge(s_back, o + 1)
                link(nc.vector.tensor_copy(carry[:, o, :], pr[:, o, 1, 0:H]))
                for h in range(H):
                    ins = nc.vector.tensor_tensor_scan(dst[:, h, way], pen[:, way], src[:, h, way], carry[:, o, h:h + 1],
                                                       ALU.add, ALU.max)
                    if o == 0:
                        link(ins)
                    else:
                        ins.then_inc(s_f, 1)
            for r in range(R):
                dve.wait_ge(s_g2, r + 1)
                at = g.L[:, P * r:P * (r + 1), :].rearrange("p s h -> p (s h)")
                nc.vector.tensor_tensor(at, at, pt[:, r % 2, :], ALU.subtract).then_inc(s_sub, 1)


def aggregate(nc, z, g, layer):
    T, HT, NS, A = 16, 8, z.NS, D + H
    with Stage(nc, f"agg{layer}") as st:
        vb = st.sb("vb", [P, 2, HT, D])
        odd = st.sb("odd", [P, z.NB, A])
        w = st.sb("w", [P, 2, HT, A])
        off = st.sb("off", [P, 2, HT, P])
        oh = st.sb("oh", [P, 2, HT, P])
        ps = st.ps("ps", [P, HT, 2 * D])
        s_vb = [st.sem(f"s_vb{h}") for h in range(2)]
        s_spare = st.sem("s_spare")
        s_wp = st.sem("s_wp")
        s_z, s_w, s_w4, s_off, s_oh, s_pe, s_acc = (
            st.sem(n) for n in ("s_z", "s_w", "s_w4", "s_off", "s_oh", "s_pe", "s_acc"))
        block = st.block()

        MINE = ((0, 3, 6), (1, 2, 4, 5, 7))

        def weigh(eng, mine, sem, i, j):
            s, h = i * T + j, j // HT
            if j % HT == MINE[mine][0]:
                eng.wait_ge(s_vb[h], 16 * i + 16)
            need(eng, s_pe, s - T + 1)
            return (nc.vector if mine == 0 else nc.gpsimd).tensor_tensor(
                w[:, h, j % HT, 0:D].rearrange("p (h c) -> p h c", h=H),
                vb[:, h, j % HT, :].rearrange("p (h c) -> p h c", h=H),
                g.L[:, bass.ds(s, 1), :].rearrange("p o h -> p (o h)").unsqueeze(2).to_broadcast([P, H, C]),
                ALU.mult).then_inc(sem, 1)

        @block.sync
        def _(sp):
            def body(i):
                for h in range(2):
                    for sem, n in ((s_w, len(MINE[0])), (s_wp, len(MINE[1]))):
                        need(sp, sem, (2 * (i - 1) + h + 1) * n)
                        sp.sem_inc(s_spare, 1)
                    sp.dma_start(vb[:, h, :, :], g.vjD[bass.ds(2 * i + h, 1)].rearrange("o p t d -> (o p) t d")).then_inc(s_vb[h], 16)
            turns(sp, NS // T, body)

        @block.scalar
        def _(act):
            def body(i):
                for h in range(2):
                    need(act, s_pe, (i - 1) * T + (h + 1) * HT)
                    nc.scalar.activation(w[:, h, :, D:A], g.L[:, bass.ds(i * T + h * HT, HT), :], ACT.Copy).then_inc(s_w4, 1)
                    for j in range(HT):
                        nc.scalar.activation(off[:, h, j, :], g.free[:, :], ACT.Abs, scale=-1.0,
                                             bias=g.relS[:, bass.ds(i * T + h * HT + j, 1)]).then_inc(s_off, 1)
                    act.wait_ge(s_off, i * T + (h + 1) * HT)
                    nc.scalar.activation(oh[:, h, :, :], off[:, h, :, :], ACT.Relu, bias=g.ones[:, 0:1], scale=-1.0).then_inc(s_oh, 1)
            turns(act, NS // T, body)

        @block.gpsimd
        def _(pool):
            nc.gpsimd.memset(odd[:, :, :], 0.0).then_inc(s_z, 1)

            def body(i):
                for h in range(2):
                    for j in MINE[1]:
                        weigh(pool, 1, s_wp, i, h * HT + j)
            turns(pool, NS // T, body)

        @block.tensor
        def _(pe):
            def body(i):
                for j in range(T):
                    s, h = i * T + j, j // HT
                    if j % HT == 0:
                        for sem in (s_w4, s_oh):
                            pe.wait_ge(sem, 2 * i + h + 1)
                    k = 0 if j % HT in MINE[0] else 1
                    pe.wait_ge((s_w, s_wp)[k], (2 * i + h) * len(MINE[k]) + MINE[k].index(j % HT) + 1)
                    need(pe, s_acc, s - HT + 1)
                    nc.tensor.matmul(ps[:, j % HT, 0:A], oh[:, h, j % HT, :], w[:, h, j % HT, :], start=True, stop=True).then_inc(s_pe, 1)
            turns(pe, NS // T, body)

        @block.vector
        def _(dve):
            nc.vector.memset(g.acc[:, :, :], 0.0).then_inc(s_z, 1)

            def blocks_of(i, h):
                return table(nc, dve, g.tab[0:1, bass.ds(z.NSP + i * T + h * HT, HT)], z.NB - 1)

            def add(i, j, b):
                s = i * T + j
                dve.wait_ge(s_pe, s + 1)
                need(dve, s_acc, s - 1)
                at = (g.acc, odd)[j % 2][:, bass.ds(b, 1), :].rearrange("p o n -> p (o n)")
                nc.vector.tensor_tensor(at, ps[:, j % HT, 0:A], at, ALU.add).then_inc(s_acc, 1)

            def body(i):
                first = isinstance(i, int) and i == 0
                before = None if first else blocks_of(i - 1, 1)
                for j in range(HT):
                    if j in MINE[0]:
                        weigh(dve, 0, s_w, i, j)
                    if not first:
                        add(i - 1, HT + j, before[j])
                here = blocks_of(i, 0)
                for j in range(HT):
                    if j in MINE[0]:
                        weigh(dve, 0, s_w, i, HT + j)
                    add(i, j, here[j])
            dve.wait_ge(s_z, 2)
            turns(dve, NS // T, body)
            last = blocks_of(NS // T - 1, 1)
            for j in range(HT):
                add(NS // T - 1, HT + j, last[j])
            dve.wait_ge(s_acc, NS)
            nc.vector.tensor_tensor(g.acc[:, :, :], g.acc[:, :, :], odd[:, :, :], ALU.add)


def finish(nc, z, g, a):
    UB, NB = z.UB, z.NB
    with Stage(nc, "fin") as st:
        Wr = st.sb("Wr", [P, 2, EX])
        br = st.sb("br", [P, EX])
        gam = st.sb("gam", [P, D])
        bet = st.sb("bet", [P, D])
        eps = st.sb("eps", [P, 1])
        sk = st.sb("sk", [P, UB, D])
        den = st.sb("den", [P, UB, H])
        rden = st.sb("rden", [P, UB, H])
        x1 = st.sb("x1", [P, UB, D])
        stat = st.sb("stat", [P, UB, 6])
        mv = st.sb("mv", [P, 2, UB, 2])
        sd = st.sb("sd", [P, 2, UB])
        rs = st.sb("rs", [P, 2, UB])
        xa = st.sb("xa", [P, UB, D])
        xn = st.sb("xn", [P, UB, D])
        xg = st.sb("xg", [P, UB, D])
        xT = st.sb("xT", [P, UB, 2, P])
        pT = st.ps("pT", [P, 2, 2 * D])
        pl = st.ps("pl", [P, 2 * D])
        s_w, s_eps, s_c, s_x1, s_mv, s_sd, s_xn, s_tr, s_xT, s_pl, s_lg, s_r, s_step = (
            st.sem(n) for n in ("s_w", "s_eps", "s_c", "s_x1", "s_mv", "s_sd", "s_xn", "s_tr", "s_xT", "s_pl", "s_lg", "s_r", "s_step"))
        s_sk = [st.sem(f"s_sk{j}") for j in range(UB)]
        s_st = [st.sem(f"s_st{j}") for j in range(UB)]
        s_sn = [st.sem(f"s_sn{j}") for j in range(UB)]
        s_raw, s_gm = st.sem("s_raw"), st.sem("s_gm")
        block = st.block()

        @block.sync
        def _(sp):
            sp.dma_start(Wr[:, :, :], a["Wr"].rearrange("(c p) n -> p c n", p=P)).then_inc(s_w, 16)
            for t, n in ((br, "br"), (gam, "gamma"), (bet, "beta")):
                sp.dma_start(t[:, :], a[n].partition_broadcast(P)).then_inc(s_w, 16)

            def body(i):
                for j in range(UB):
                    b = i * UB + j
                    need(sp, s_x1, b - UB + 1)
                    sp.dma_start(sk[:, j, :], g.skipD[bass.ds(b * P, P), :]).then_inc(s_sk[j], 16)
            turns(sp, NB // UB, body)

        @block.scalar
        def _(act):
            act.wait_ge(s_eps, 1)

            def deviation(i, o):
                act.wait_ge(s_mv, 2 * i + o + 1)
                nc.scalar.activation(sd[:, o, :], mv[:, o, :, 1], ACT.Sqrt, bias=eps[:, 0:1]).then_inc(s_sd, 1)

            def tail(i):
                for j in range(UB):
                    b = i * UB + j
                    act.wait_ge(s_tr, b + 1)
                    need(act, s_pl, b - UB + 1)
                    nc.scalar.activation(xT[:, j, :, :], pT[:, j % 2, 0:D].rearrange("p (c m) -> p c m", c=2), ACT.Copy).then_inc(s_xT, 1)
                    act.dma_start(g.xnD[bass.ds(b * P, P), :], xg[:, j, :]).then_inc(s_sn[j], 16)

            def body(i):
                deviation(i, 0)
                for j in range(UB):
                    b = i * UB + j
                    act.wait_ge(s_x1, b + 1)
                    act.dma_start(g.x1D[bass.ds(b * P, P), :], x1[:, j, :]).then_inc(s_st[j], 16)
                deviation(i, 1)
                if not isinstance(i, int) or i > 0:
                    tail(i - 1)
            turns(act, NB // UB, body, peel=2)
            tail(NB // UB - 1)
            for j in range(UB):
                act.wait_ge(s_st[j], 16 * (NB // UB))
                act.wait_ge(s_sn[j], 16 * (NB // UB))

        @block.gpsimd
        def _(pool):
            pool.wait_ge(s_w, 64)

            def body(i):
                for j in range(UB):
                    b = i * UB + j
                    pool.wait_ge(s_raw, b + 1)
                    need(pool, s_tr, b - UB + 1)
                    need(pool, s_sn[j], 16 * i)
                    nc.gpsimd.tensor_tensor(xg[:, j, :], xn[:, j, :], gam[:, :], ALU.mult).then_inc(s_gm, 1)
                    if j > 0:
                        pool.wait_ge(s_gm, b)
                        nc.gpsimd.tensor_tensor(xg[:, j - 1, :], xg[:, j - 1, :], bet[:, :], ALU.add).then_inc(s_xn, 1)
                pool.wait_ge(s_gm, (i + 1) * UB)
                nc.gpsimd.tensor_tensor(xg[:, UB - 1, :], xg[:, UB - 1, :], bet[:, :], ALU.add).then_inc(s_xn, 1)
            turns(pool, NB // UB, body)

        @block.tensor
        def _(pe):
            pe.wait_ge(s_w, 64)

            def body(i):
                for j in range(UB + 1):
                    if j < UB:
                        b = i * UB + j
                        pe.wait_ge(s_xn, b + 1)
                        need(pe, s_xT, b - back(j, 2, UB) + 1)
                        for c in range(2):
                            ins = nc.tensor.transpose(pT[:, j % 2, c * P:(c + 1) * P], xg[:, j, c * P:(c + 1) * P], g.ident[:, :])
                        ins.then_inc(s_tr, 1)
                    if j > 0:
                        u, b = j - 1, i * UB + j - 1
                        pe.wait_ge(s_xT, b + 1)
                        if u == 0:
                            need(pe, s_lg, i)
                        for c in range(2):
                            ins = nc.tensor.matmul(pl[:, u * EX:(u + 1) * EX], xT[:, u, c, :], Wr[:, c, :], start=(c == 0), stop=(c == 1))
                        ins.then_inc(s_pl, 1)
            turns(pe, NB // UB, body)

        @block.vector
        def _(dve):
            nc.vector.memset(eps[:, :], EPS).then_inc(s_eps, 1)
            dve.wait_ge(s_w, 64)
            PER = 2 + 4 * UB

            def router(i):
                dve.wait_ge(s_pl, (i + 1) * UB)
                nc.vector.tensor_tensor(g.lg[:, bass.ds(i * UB, UB), :], pl[:, 0:UB * EX].rearrange("p (b e) -> p b e", e=EX),
                                        br[:, :].unsqueeze(1).to_broadcast([P, UB, EX]), ALU.add).then_inc(s_lg, 1)

            def body(i):
                n = [0]

                def link(ins):
                    n[0] += 1
                    ins.then_inc(s_c, 1)

                def seen():
                    dve.wait_ge(s_c, i * PER + n[0])

                at = g.acc[:, bass.ds(i * UB, UB), :]
                link(nc.vector.tensor_scalar(den[:, :, :], at[:, :, D:D + H], 1e-16, None, ALU.add))
                seen()
                link(nc.vector.reciprocal(rden[:, :, :], den[:, :, :]))
                seen()
                for j in range(UB):
                    need(dve, s_st[j], 16 * i)
                    link(nc.vector.tensor_tensor(x1[:, j, :].rearrange("p (h c) -> p h c", h=H),
                                                 at[:, j, 0:D].rearrange("p (h c) -> p h c", h=H),
                                                 rden[:, j, :].unsqueeze(2).to_broadcast([P, H, C]), ALU.mult))
                seen()
                for j in range(UB):
                    dve.wait_ge(s_sk[j], 16 * i + 16)
                    nc.vector.tensor_tensor(x1[:, j, :], x1[:, j, :], sk[:, j, :], ALU.add).then_inc(s_x1, 1)
                dve.wait_ge(s_x1, (i + 1) * UB)
                for o, (src, dst) in enumerate(((x1, xa), (xa, xn))):
                    for j in range(UB):
                        link(nc.vector.bn_stats(stat[:, j, :], src[:, j, :]))
                    seen()
                    dve.sem_inc(s_step, 1)
                    for j in range(UB):
                        ins = nc.vector.bn_aggr(mv[:, o, j, :], stat[:, j, :])
                    ins.then_inc(s_mv, 1)
                    dve.wait_ge(s_sd, 2 * i + o + 1)
                    nc.vector.reciprocal(rs[:, o, :], sd[:, o, :]).then_inc(s_r, 1)
                    dve.wait_ge(s_r, 2 * i + o + 1)
                    for j in range(UB):
                        if o == 1:
                            need(dve, s_gm, i * UB + j - UB + 1)
                        ins = nc.vector.tensor_scalar(dst[:, j, :], src[:, j, :], mv[:, o, j, 0:1], rs[:, o, j:j + 1],
                                                      ALU.subtract, ALU.mult)
                        if o == 0:
                            link(ins)
                        else:
                            ins.then_inc(s_raw, 1)
                    if o == 0:
                        seen()
                if not isinstance(i, int) or i > 0:
                    router(i - 1)
                assert n[0] == PER, n[0]
            turns(dve, NB // UB, body)
            router(NB // UB - 1)


def route(nc, z, g, a):
    NB, NE = z.NB, z.NE
    with Stage(nc, "route") as st:
        top = st.sb("top", [P, NB, 8])
        idx = st.sb("idx", [P, NB, 8], U32)
        pick = st.sb("pick", [P, 2, NB])
        dif = st.sb("dif", [P, NB])
        ex = st.sb("ex", [P, NB])
        ex1 = st.sb("ex1", [P, NB])
        e8i = st.sb("e8i", [P, EX], I32)
        e8 = st.sb("e8", [P, EX])
        tri = st.sb("tri", [P, P])
        O = st.sb("O", [P, 2, NB, EX])
        both = st.sb("both", [P, NB, EX])
        tot = st.sb("tot", [P, NB, EX])
        inc = st.sb("inc", [P, NB, EX])
        place = st.sb("place", [P, NB, EX])
        cnt = st.sb("cnt", [P, EX])
        cnti = st.sb("cnti", [P, EX], I32)
        tl = st.sb("tl", [P, EX])
        end = st.sb("end", [P, EX])
        off = st.sb("off", [P, EX])
        tmp = st.sb("tmp", [P, NB, EX])
        posf = st.sb("posf", [P, 2, NB])
        ti = st.sb("ti", [P, NE], I32)
        tf = st.sb("tf", [P, NE])
        ge = st.sb("ge", [P, NE])
        et = st.sb("et", [P, NE])
        onesb = st.sb("onesb", [P, NB])
        pr = st.ps("pr", [P, 2, 2 * D])
        s_w = st.sem("s_w")
        s_io, s_c, s_dif, s_exp, s_O, s_mm = (
            st.sem(n) for n in ("s_io", "s_c", "s_dif", "s_exp", "s_O", "s_mm"))
        block = st.block()

        @block.gpsimd
        def _(pool):
            nc.gpsimd.iota(e8i[:, :], [[1, EX]], base=0, channel_multiplier=0).then_inc(s_io, 1)
            nc.gpsimd.iota(ti[:, :], [[1, NE]], base=0, channel_multiplier=0).then_inc(s_io, 1)

        @block.scalar
        def _(act):
            act.wait_ge(s_dif, 1)
            nc.scalar.activation(ex[:, :], dif[:, :], ACT.Exp).then_inc(s_exp, 1)

        @block.sync
        def _(sp):
            for e in range(EX):
                sp.dma_start(g.W1[:, e, :, :], a["W1"][e].rearrange("(c p) n -> p c n", p=P)).then_inc(s_w, 16)
            sp.dma_start(g.b1[:, :, :].rearrange("p e n -> p (e n)"), a["b1"].rearrange("e n -> (e n)").partition_broadcast(P)).then_inc(s_w, 16)
            sp.dma_start(g.b2[:, :, :].rearrange("p e n -> p (e n)"), a["b2"].rearrange("e n -> (e n)").partition_broadcast(P)).then_inc(s_w, 16)
            sp.wait_ge(s_w, 16 * (EX + 2))

        @block.tensor
        def _(pe):
            pe.wait_ge(s_O, 1)
            flat = both[:, :, :].rearrange("p b e -> p (b e)")
            nc.tensor.matmul(pr[:, 0, 0:NB * EX], tri[:, :], flat, start=True, stop=True)
            nc.tensor.matmul(pr[:, 1, 0:NB * EX], g.ones[:, :], flat, start=True, stop=True).then_inc(s_mm, 1)

        @block.vector
        def _(dve):
            n = [0]

            def link(ins):
                n[0] += 1
                ins.then_inc(s_c, 1)
                dve.wait_ge(s_c, n[0])

            link(nc.vector.tensor_scalar(tri[:, :], g.free[:, :], g.part[:, 0:1], None, ALU.is_gt))
            link(nc.vector.memset(onesb[:, :], 1.0))
            for b in range(NB):
                nc.vector.max(top[:, b, :], g.lg[:, b, :]).then_inc(s_c, 1)
            n[0] += NB
            dve.wait_ge(s_c, n[0])
            for b in range(NB):
                nc.vector.max_index(idx[:, b, :], top[:, b, :], g.lg[:, b, :]).then_inc(s_c, 1)
            n[0] += NB
            dve.wait_ge(s_c, n[0])
            nc.vector.tensor_tensor(dif[:, :], top[:, :, 1], top[:, :, 0], ALU.subtract).then_inc(s_dif, 1)
            for k in range(2):
                link(nc.vector.tensor_copy(pick[:, k, :], idx[:, :, k]))
            dve.wait_ge(s_io, 2)
            link(nc.vector.tensor_copy(e8[:, :], e8i[:, :]))
            for k in range(2):
                link(nc.vector.tensor_tensor(O[:, k, :, :], pick[:, k, :].unsqueeze(2).to_broadcast([P, NB, EX]),
                                             e8[:, :].unsqueeze(1).to_broadcast([P, NB, EX]), ALU.is_equal))
            nc.vector.tensor_tensor(both[:, :, :], O[:, 0, :, :], O[:, 1, :, :], ALU.add).then_inc(s_O, 1)
            dve.wait_ge(s_exp, 1)
            link(nc.vector.tensor_scalar(ex1[:, :], ex[:, :], 1.0, None, ALU.add))
            link(nc.vector.reciprocal(g.wt[:, 0, :], ex1[:, :]))
            link(nc.vector.tensor_tensor(g.wt[:, 1, :], ex[:, :], g.wt[:, 0, :], ALU.mult))
            dve.wait_ge(s_mm, 1)
            link(nc.vector.tensor_copy(tot[:, :, :], pr[:, 1, 0:NB * EX].rearrange("p (b e) -> p b e", e=EX)))
            for e in range(EX):
                link(nc.vector.tensor_tensor_scan(inc[:, :, e], onesb[:, :], tot[:, :, e], 0.0, ALU.mult, ALU.add))
            link(nc.vector.tensor_copy(cnt[:, :], inc[:, NB - 1, :]))
            link(nc.vector.tensor_tensor(inc[:, :, :], inc[:, :, :], tot[:, :, :], ALU.subtract))
            link(nc.vector.tensor_tensor(place[:, :, :], inc[:, :, :], pr[:, 0, 0:NB * EX].rearrange("p (b e) -> p b e", e=EX), ALU.add))
            link(nc.vector.tensor_scalar(cnti[:, :], cnt[:, :], float(P - 1), None, ALU.add))
            link(nc.vector.tensor_scalar(cnti[:, :], cnti[:, :], 7, None, ALU.arith_shift_right))
            link(nc.vector.tensor_copy(tl[:, :], cnti[:, :]))
            link(nc.vector.tensor_tensor_scan(end[:, :], g.ones[:, 0:EX], tl[:, :], 0.0, ALU.mult, ALU.add))
            link(nc.vector.tensor_tensor(off[:, :], end[:, :], tl[:, :], ALU.subtract))
            link(nc.vector.tensor_scalar(off[:, :], off[:, :], float(P), None, ALU.mult))
            link(nc.vector.tensor_tensor(place[:, :, :], place[:, :, :], off[:, :].unsqueeze(1).to_broadcast([P, NB, EX]), ALU.add))
            for k in range(2):
                link(nc.vector.tensor_tensor(tmp[:, :, :], O[:, k, :, :], place[:, :, :], ALU.mult))
                link(nc.vector.tensor_reduce(posf[:, k, :], tmp[:, :, :], AX, ALU.add))
            link(nc.vector.tensor_copy(g.pos[:, :, :].rearrange("p b k -> p k b"), posf[:, :, :]))
            link(nc.vector.tensor_copy(tf[:, :], ti[:, :]))
            link(nc.vector.memset(et[:, :], 0.0))
            for e in range(EX - 1):
                link(nc.vector.tensor_scalar(ge[:, :], tf[:, :], end[:, e:e + 1], None, ALU.is_ge))
                link(nc.vector.tensor_tensor(et[:, :], et[:, :], ge[:, :], ALU.add))
            nc.vector.tensor_copy(g.etab[:, :], et[0:1, :])


def dispatch(nc, z, g, a):
    UB, NB = z.UB, z.NB
    with Stage(nc, "disp") as st:
        xr = st.sb("xr", [P, UB, D])
        ix = st.sb("ix", [P, UB, 2], I32)
        s_x = [st.sem(f"s_x{j}") for j in range(UB)]
        s_sc = [st.sem(f"s_sc{j}") for j in range(UB)]
        s_ix, s_step, s_w = st.sem("s_ix"), st.sem("s_step"), st.sem("s_w")
        block = st.block()

        @block.scalar
        def _(act):
            for e in range(EX):
                act.dma_start(g.W2[:, e, :, :], a["W2"][e].rearrange("(c p) n -> p c n", p=P)).then_inc(s_w, 16)
            act.wait_ge(s_w, 16 * EX)

        @block.sync
        def _(sp):
            def body(i):
                for j in range(UB):
                    need(sp, s_sc[j], 32 * i)
                    sp.dma_start(xr[:, j, :], g.xnD[bass.ds((i * UB + j) * P, P), :]).then_inc(s_x[j], 16)
            turns(sp, NB // UB, body)

        @block.gpsimd
        def _(pool):
            def body(i):
                for j in range(UB):
                    need(pool, s_sc[j], 32 * i)
                nc.gpsimd.tensor_copy(ix[:, :, :], g.pos[:, bass.ds(i * UB, UB), :]).then_inc(s_ix, 1)
                pool.wait_ge(s_ix, i + 1)
                for j in range(UB):
                    pool.wait_ge(s_x[j], 16 * i + 16)
                    pool.sem_inc(s_step, 1)
                    for k in range(2):
                        nc.gpsimd.indirect_dma_start(
                            out=g.xsD, out_offset=bass.IndirectOffsetOnAxis(ap=ix[:, j, k:k + 1].bitcast(U32), axis=0),
                            in_=xr[:, j, :], in_offset=None).then_inc(s_sc[j], 16)
            turns(pool, NB // UB, body)
            for j in range(UB):
                pool.wait_ge(s_sc[j], 32 * (NB // UB))


def experts(nc, z, g, a):
    UE, NE, KH = 6, z.NE, HID // P
    with Stage(nc, "exp") as st:
        xr = st.sb("xr", [P, UE, D])
        xT = st.sb("xT", [P, 2, D])
        hb = st.sb("hb", [P, 2, HID])
        hg = st.sb("hg", [P, 2, HID])
        hT = st.sb("hT", [P, 2, HID])
        yo = st.sb("yo", [P, UE, D])
        pX = st.ps("pX", [P, 2, 2 * D])
        pH = st.ps("pH", [P, 2, HID])
        pT = st.ps("pT", [P, 2, HID])
        pY = st.ps("pY", [P, 2, 2 * D])
        s_tx, s_xT, s_h, s_hb, s_hg, s_th, s_hT, s_y, s_yo = (
            st.sem(n) for n in ("s_tx", "s_xT", "s_h", "s_hb", "s_hg", "s_th", "s_hT", "s_y", "s_yo"))
        s_x = [st.sem(f"s_x{j}") for j in range(UE)]
        s_st = [st.sem(f"s_st{j}") for j in range(UE)]
        block = st.block()
        n_turns = NE // UE

        def piped(eng, stages):
            deep = max(d for d, _ in stages)

            def body(i):
                for j in range(UE):
                    for d, f in stages:
                        if j >= d:
                            f(i, j - d)
                        elif not isinstance(i, int) or i > 0:
                            f(i - 1, j - d + UE)
            turns(eng, n_turns, body, peel=2)
            for j in range(deep):
                for d, f in stages:
                    if j < d:
                        f(n_turns - 1, j - d + UE)

        @block.sync
        def _(sp):
            def body(i):
                for j in range(UE):
                    t = i * UE + j
                    need(sp, s_tx, t - UE + 1)
                    sp.dma_start(xr[:, j, :], g.xsD[bass.ds(t * P, P), :]).then_inc(s_x[j], 16)
            turns(sp, n_turns, body)

        @block.tensor
        def _(pe):
            def expert(t):
                return pe.value_load(g.etab[0:1, bass.ds(t, 1)], min_val=0, max_val=EX - 1)

            def x_transpose(i, j):
                t = i * UE + j
                pe.wait_ge(s_x[j], 16 * i + 16)
                need(pe, s_xT, t - 1)
                for c in range(2):
                    ins = nc.tensor.transpose(pX[:, j % 2, c * P:(c + 1) * P], xr[:, j, c * P:(c + 1) * P], g.ident[:, :])
                ins.then_inc(s_tx, 1)

            def first(i, j):
                t = i * UE + j
                e = expert(t)
                pe.wait_ge(s_xT, t + 1)
                need(pe, s_hb, t - 1)
                for c in range(2):
                    ins = nc.tensor.matmul(pH[:, j % 2, :], xT[:, j % 2, c * P:(c + 1) * P],
                                           g.W1[:, bass.ds(e, 1), c, :].rearrange("p o n -> p (o n)"), start=(c == 0), stop=(c == 1))
                ins.then_inc(s_h, 1)

            def h_transpose(i, j):
                t = i * UE + j
                pe.wait_ge(s_hg, t + 1)
                need(pe, s_hT, t - 1)
                for c in range(KH):
                    ins = nc.tensor.transpose(pT[:, j % 2, c * P:(c + 1) * P], hg[:, j % 2, c * P:(c + 1) * P], g.ident[:, :])
                ins.then_inc(s_th, 1)

            def second(i, j):
                t = i * UE + j
                e = expert(t)
                pe.wait_ge(s_hT, t + 1)
                need(pe, s_yo, t - 1)
                for c in range(KH):
                    ins = nc.tensor.matmul(pY[:, j % 2, 0:D], hT[:, j % 2, c * P:(c + 1) * P],
                                           g.W2[:, bass.ds(e, 1), c, :].rearrange("p o n -> p (o n)"), start=(c == 0), stop=(c == KH - 1))
                ins.then_inc(s_y, 1)
            piped(pe, ((0, x_transpose), (1, first), (2, h_transpose), (3, second)))

        @block.scalar
        def _(act):
            def x_copy(i, j):
                t = i * UE + j
                act.wait_ge(s_tx, t + 1)
                need(act, s_h, t - 1)
                nc.scalar.activation(xT[:, j % 2, :], pX[:, j % 2, 0:D], ACT.Copy).then_inc(s_xT, 1)

            def gelu(i, j):
                t = i * UE + j
                act.wait_ge(s_hb, t + 1)
                need(act, s_th, t - 1)
                nc.scalar.activation(hg[:, j % 2, :], hb[:, j % 2, :], ACT.Gelu).then_inc(s_hg, 1)

            def h_copy(i, j):
                t = i * UE + j
                act.wait_ge(s_th, t + 1)
                need(act, s_y, t - 1)
                nc.scalar.activation(hT[:, j % 2, :], pT[:, j % 2, :], ACT.Copy).then_inc(s_hT, 1)

            def store(i, j):
                act.wait_ge(s_yo, i * UE + j + 1)
                act.dma_start(g.ysD[bass.ds((i * UE + j) * P, P), :], yo[:, j, :]).then_inc(s_st[j], 16)
            piped(act, ((0, x_copy), (1, gelu), (2, h_copy), (4, store)))
            for j in range(UE):
                act.wait_ge(s_st[j], 16 * n_turns)

        @block.vector
        def _(dve):
            def bias1(i, j):
                t = i * UE + j
                e = dve.value_load(g.etab[0:1, bass.ds(t, 1)], min_val=0, max_val=EX - 1)
                dve.wait_ge(s_h, t + 1)
                need(dve, s_hg, t - 1)
                nc.vector.tensor_tensor(hb[:, j % 2, :], pH[:, j % 2, :], g.b1[:, bass.ds(e, 1), :].rearrange("p o n -> p (o n)"),
                                        ALU.add).then_inc(s_hb, 1)

            def bias2(i, j):
                t = i * UE + j
                e = dve.value_load(g.etab[0:1, bass.ds(t, 1)], min_val=0, max_val=EX - 1)
                dve.wait_ge(s_y, t + 1)
                need(dve, s_st[j], 16 * i)
                nc.vector.tensor_tensor(yo[:, j, :], pY[:, j % 2, 0:D], g.b2[:, bass.ds(e, 1), :].rearrange("p o n -> p (o n)"),
                                        ALU.add).then_inc(s_yo, 1)
            piped(dve, ((1, bias1), (3, bias2)))


def combine(nc, z, g, out):
    UB, NB = z.UB, z.NB
    with Stage(nc, "comb") as st:
        yr = st.sb("yr", [P, UB, 2, D])
        x1 = st.sb("x1", [P, UB, D])
        xo = st.sb("xo", [P, UB, D])
        ix = st.sb("ix", [P, 2, UB, 2], I32)
        s_y = [st.sem(f"s_y{j}") for j in range(UB)]
        s_x = [st.sem(f"s_x{j}") for j in range(UB)]
        s_st = [st.sem(f"s_st{j}") for j in range(UB)]
        s_ix, s_step, s_t, s_o = (st.sem(n) for n in ("s_ix", "s_step", "s_t", "s_o"))
        block = st.block()

        @block.sync
        def _(sp):
            def body(i):
                for j in range(UB):
                    b = i * UB + j
                    need(sp, s_t, b - UB + 1)
                    sp.dma_start(x1[:, j, :], g.x1D[bass.ds(b * P, P), :]).then_inc(s_x[j], 16)
            turns(sp, NB // UB, body)

        @block.gpsimd
        def _(pool):
            def body(i):
                need(pool, s_o, (i - 1) * UB + UB)
                nc.gpsimd.tensor_copy(ix[:, 0, :, :], g.pos[:, bass.ds(i * UB, UB), :]).then_inc(s_ix, 1)
                pool.wait_ge(s_ix, i + 1)
                pool.sem_inc(s_step, 1)
                for j in range(UB):
                    for k in range(2):
                        nc.gpsimd.indirect_dma_start(
                            out=yr[:, j, k, :], out_offset=None, in_=g.ysD,
                            in_offset=bass.IndirectOffsetOnAxis(ap=ix[:, 0, j, k:k + 1].bitcast(U32), axis=0),
                        ).then_inc(s_y[j], 16)
            turns(pool, NB // UB, body)

        @block.scalar
        def _(act):
            def body(i):
                for j in range(UB):
                    b = i * UB + j
                    act.wait_ge(s_o, b + 1)
                    act.dma_start(out[bass.ds(b * P, P), :], xo[:, j, :]).then_inc(s_st[j], 16)
            turns(act, NB // UB, body)
            for j in range(UB):
                act.wait_ge(s_st[j], 16 * (NB // UB))

        @block.vector
        def _(dve):
            def body(i):
                for j in range(UB):
                    b = i * UB + j
                    dve.wait_ge(s_y[j], 32 * i + 32)
                    dve.wait_ge(s_x[j], 16 * i + 16)
                    need(dve, s_st[j], 16 * i)
                    nc.vector.scalar_tensor_tensor(out=xo[:, j, :], in0=yr[:, j, 0, :], scalar=g.wt[:, 0, bass.ds(b, 1)],
                                                   in1=x1[:, j, :], op0=ALU.mult, op1=ALU.add).then_inc(s_t, 1)
                    dve.wait_ge(s_t, b + 1)
                    nc.vector.scalar_tensor_tensor(out=xo[:, j, :], in0=yr[:, j, 1, :], scalar=g.wt[:, 1, bass.ds(b, 1)],
                                                   in1=xo[:, j, :], op0=ALU.mult, op1=ALU.add).then_inc(s_o, 1)
            turns(dve, NB // UB, body)


GNN = [w + n for n in "12" for w in ("Wq", "bq", "Wk", "bk", "Wv", "bv", "We", "Ws", "bs")]


def build(nc, z, a, out):
    g = Record()

    def dram(name, shape, dt=F32):
        return nc.dram_tensor(name, shape, dt, kind="Internal").ap()

    def keep(ctx, name, shape, dt=F32):
        return ctx.enter_context(nc.sbuf_tensor(name, shape, dt))

    NP = z.NB * P
    g.tabD = dram("tabD", (2, z.NSP), I32)
    g.relD = dram("relD", (z.NSP, P), U8)
    g.keyD = dram("keyD", (z.NSP * P + 2,))
    g.xTD = dram("xTD", (NP, D))
    g.kvD = dram("kvD", (NP, 2 * D))
    g.baseD = dram("baseD", (NP, D))
    g.resD = dram("resD", (NP, D))
    g.skipD = dram("skipD", (NP, D))
    g.vjD = dram("vjD", (z.NS // 8, P, 8, D))
    g.LD = dram("LD", (z.NSP, H, P))
    g.GD = dram("GD", (z.NSP, H, P))
    g.x1D = dram("x1D", (NP, D))
    g.xnD = dram("xnD", (NP, D))
    g.xsD = dram("xsD", (z.NE * P, D))
    g.ysD = dram("ysD", (z.NE * P, D))
    with ExitStack() as whole:
        g.ident = keep(whole, "ident", [P, P])
        g.part = keep(whole, "part", [P, 1])
        g.free = keep(whole, "free", [P, P])
        g.ones = keep(whole, "ones", [P, P])
        g.lg = keep(whole, "lg", [P, z.NB, EX])
        g.pos = keep(whole, "pos", [P, z.NB, 2], I32)
        g.wt = keep(whole, "wt", [P, 2, z.NB])
        g.etab = keep(whole, "etab", [1, z.NE], I32)
        constants(nc, g)
        with ExitStack() as edges:
            g.tab = keep(edges, "tab", [1, 2 * z.NSP], I32)
            g.srcS = keep(edges, "srcS", [P, z.NSP], I32)
            g.relS = keep(edges, "relS", [P, z.NSP])
            g.pen_prev = keep(edges, "pen_prev", [P, z.U * P])
            g.pen_next = keep(edges, "pen_next", [P, z.U * P])
            g.pen_row = keep(edges, "pen_row", [H, 2, P])
            plan(nc, z, g, a["src_t"], a["dst_t"], a["dst_first"])
            g.acc = keep(edges, "acc", [P, z.NB, D + H])
            with Stage(nc, "mixkv") as st:
                g.kTm, g.vm = st.sb("kTm", [P, NP]), st.sb("vm", [P, NP])
                nodes(nc, z, g, 1, a)
                mix(nc, z, g, a)
            g.L = keep(edges, "L", [P, z.NSP, H])
            for layer in (1, 2):
                if layer == 2:
                    nodes(nc, z, g, 2, a)
                logits(nc, z, g, layer, a)
                seg_max(nc, z, g, layer)
                aggregate(nc, z, g, layer)
            finish(nc, z, g, a)
        g.W1 = keep(whole, "W1", [P, EX, D // P, HID])
        g.W2 = keep(whole, "W2", [P, EX, HID // P, D])
        g.b1 = keep(whole, "b1", [P, EX, HID])
        g.b2 = keep(whole, "b2", [P, EX, D])
        route(nc, z, g, a)
        dispatch(nc, z, g, a)
        experts(nc, z, g, a)
        combine(nc, z, g, out)


def kernel(**inputs):
    import numpy as np
    import concourse.bacc as bacc
    from concourse.bass_utils import run_bass_kernel_spmd as run

    x, src, dst, ea = (np.asarray(inputs[n]) for n in ("x", "src", "dst", "edge_attr_194"))
    z = sizes(x.shape[0], src.shape[0])
    pad = z.NT * P - z.E
    lay = {
        "x": np.pad(x, ((0, z.NB * P - z.N), (0, 0))),
        "src_t": np.pad(src, (0, pad)).reshape(z.NT, P),
        "dst_t": np.pad(dst, (0, pad), constant_values=z.NB * P - 1).reshape(z.NT, P),
        "ea_t": np.ascontiguousarray(np.pad(ea, ((0, pad), (0, 0))).reshape(z.NT, P, 2, EK).transpose(0, 3, 2, 1)).reshape(z.NT, EK, 2 * P),
    }
    lay["dst_first"] = np.ascontiguousarray(lay["dst_t"][:, 0])
    for n in GNN:
        lay[n] = np.asarray(inputs["L0_gnn_" + n])
    lay["W_qkv"] = np.asarray(inputs["L0_mix_W_qkv"])
    lay["Wq_mix_T"] = np.ascontiguousarray(lay["W_qkv"][:, :MH].T)
    lay["W_out"] = np.asarray(inputs["L0_mix_W_out"])
    lay["b_out"] = np.asarray(inputs["L0_mix_b_out"])
    for n in ("gamma", "beta", "Wr", "br", "W1", "b1", "W2", "b2"):
        lay[n] = np.asarray(inputs["L0_ffn_" + n])
    nc = bacc.Bacc("TRN2", target_bir_lowering=False, num_devices=1)
    arrays, a = {}, {}
    for n, v in lay.items():
        arrays[n + "_dram"] = v
        a[n] = nc.dram_tensor(n + "_dram", v.shape, mybir.dt.from_np(v.dtype), kind="ExternalInput").ap()
    out = nc.dram_tensor("out_dram", (z.NB * P, D), F32, kind="ExternalOutput").ap()
    build(nc, z, a, out)
    return run(nc, [arrays], core_ids=[0]).results[0]["out_dram"][:z.N]
```
